# Optimizing a Trainium2 kernel written in Bass

```python
import numpy as np
import jax
import jax.numpy as jnp

def _softmax(x, axis=-1):
    return jax.nn.softmax(x, axis=axis)

def _gelu(x):
    return jax.nn.gelu(x, approximate=True)

def _silu(x):
    return jax.nn.silu(x)

def _sigmoid(x):
    return jax.nn.sigmoid(x)

def _layernorm(x, axis=-1, eps=1e-05):
    m = jnp.mean(x, axis=axis, keepdims=True)
    v = jnp.var(x, axis=axis, keepdims=True)
    return (x - m) / jnp.sqrt(v + eps)

def _scatter_add(tgt, idx, src, axis=0):
    return tgt.at[idx].add(src)

def _segment_sum(src, seg, n):
    return jax.ops.segment_sum(src, seg, n)
kernel_name = 'mk_decoder_postln_d1_seqx_r2_dc2866'

def setup_inputs(seed: int=0):
    np.random.seed(seed)
    _w = jnp.asarray

    def _rec_inputs():
        import jax
        import jax.numpy as jnp
        _rk = jax.random.key(seed)
        x = -0.000125 + 0.9999 * jax.random.normal(jax.random.fold_in(_rk, 1), (16, 256, 512), jnp.float32)
        _lenS = 256 - jax.random.randint(jax.random.fold_in(_rk, 7), (16,), 0, max(1, 256 // 4) + 1, jnp.int32)
        _lenS2 = 256 - jax.random.randint(jax.random.fold_in(_rk, 8), (16,), 0, max(1, 256 // 4) + 1, jnp.int32)
        _ctx_1024P = jax.random.normal(jax.random.fold_in(_rk, 11), (16, 16, 512), jnp.float32)
        _ctx_1024c = jax.random.dirichlet(jax.random.fold_in(_rk, 511), 0.3 * jnp.ones((16,), jnp.float32), (16, 256))
        _ctx_1024t = jnp.einsum('bsk,bkd->bsd', _ctx_1024c, _ctx_1024P)
        _ctx_1024t = _ctx_1024t * jax.lax.rsqrt(jnp.mean(jnp.square(_ctx_1024t)) + 1e-12) * 0.953939
        ctx_1024 = -1.52775e-05 + 0.999936 * (_ctx_1024t + 0.3 * jax.random.normal(jax.random.fold_in(_rk, 611), (16, 256, 512), jnp.float32))
        return (x, ctx_1024)
    x, ctx_1024 = _rec_inputs()

    def _L0_attn_setup():
        import jax, jax.numpy as jnp
        import numpy as np
        import math
        B, L, HID, NH = (4, 2048, 512, 8)
        DH = HID // NH
        THETA = 10000.0

        def _rope_tables(seq_len, dh):
            half = dh // 2
            inv_freq = 1.0 / THETA ** (jnp.arange(half, dtype=jnp.float32) / half)
            freqs = jnp.arange(seq_len, dtype=jnp.float32)[:, None] * inv_freq[None, :]
            return (jnp.cos(freqs), jnp.sin(freqs))

        def _apply_rope(x, cos, sin):
            half = x.shape[-1] // 2
            x1, x2 = (x[..., :half], x[..., half:2 * half])
            c = cos[None, None]
            s = sin[None, None]
            return jnp.concatenate([x1 * c - x2 * s, x1 * s + x2 * c], axis=-1)
        key = jax.random.key(seed)
        ks = jax.random.split(key, 9)

        def xav(k, sh):
            lim = math.sqrt(6.0 / (sh[0] + sh[1]))
            return jax.random.uniform(k, sh, jnp.float32, -lim, lim)
        return {'x': jax.random.normal(ks[0], (B, L, HID), jnp.float32), 'norm_w': jnp.ones((HID,), jnp.float32), 'Wq': xav(ks[1], (HID, HID)), 'Wk': xav(ks[2], (HID, HID)), 'Wv': xav(ks[3], (HID, HID)), 'Wbeta': xav(ks[4], (NH, HID)), 'bbeta': jnp.full((NH,), 2.0, jnp.float32), 'Wig': xav(ks[5], (NH, HID)), 'big': jnp.zeros((NH,), jnp.float32), 'Wog': xav(ks[6], (NH, HID)), 'bog': jnp.zeros((NH,), jnp.float32), 'Wout': xav(ks[7], (HID, HID)), 'bout': jnp.zeros((HID,), jnp.float32)}
    _L0_attn_all = _L0_attn_setup()
    _L0_attn_in = {k: v for k, v in _L0_attn_all.items() if k in ('norm_w', 'Wq', 'Wk', 'Wv', 'Wbeta', 'bbeta', 'Wig', 'big', 'Wog', 'bog', 'Wout', 'bout')}
    del _L0_attn_all

    def _L0_xattn_setup():
        import jax, jax.numpy as jnp
        import numpy as np
        DECAY = 0.9
        key = jax.random.key(seed)
        k1, k2, k3 = jax.random.split(key, 3)
        B, S, D = (8, 2048, 512)
        q = jax.random.normal(k1, (B, S, D), dtype=jnp.float32)
        k = jax.random.normal(k2, (B, S, D), dtype=jnp.float32)
        v = jax.random.normal(k3, (B, S, D), dtype=jnp.float32)
        return {'q': q, 'k': k, 'v': v}
    _L0_xattn_all = _L0_xattn_setup()
    _L0_xattn_in = {k: v for k, v in _L0_xattn_all.items() if k in ()}
    del _L0_xattn_all

    def _L0_ffn_setup():
        import jax, jax.numpy as jnp
        import numpy as np
        MICRO_BATCHES = 4
        NUM_EXPERTS = 8
        EPS = 1e-05
        key = jax.random.key(seed)
        ks = jax.random.split(key, 8)
        B, S, D = (8, 1024, 512)
        E, F = (NUM_EXPERTS, 4 * D)
        x = jax.random.normal(ks[0], (B, S, D), dtype=jnp.float32)
        gamma = jnp.ones((D,), jnp.float32)
        beta = jnp.zeros((D,), jnp.float32)
        gate_w = jax.random.normal(ks[1], (E, D), jnp.float32) * (1.0 / np.sqrt(D))
        w1 = jax.random.normal(ks[2], (E, D, F), jnp.float32) * (1.0 / np.sqrt(D))
        b1 = jnp.zeros((E, F), jnp.float32)
        w2 = jax.random.normal(ks[3], (E, F, D), jnp.float32) * (1.0 / np.sqrt(F))
        b2 = jnp.zeros((E, D), jnp.float32)
        return {'x': x, 'gamma': gamma, 'beta': beta, 'gate_w': gate_w, 'w1': w1, 'b1': b1, 'w2': w2, 'b2': b2}
    _L0_ffn_all = _L0_ffn_setup()
    _L0_ffn_in = {k: v for k, v in _L0_ffn_all.items() if k in ('gamma', 'beta', 'gate_w', 'w1', 'b1', 'w2', 'b2')}
    del _L0_ffn_all
    return {'x': x, 'ctx_1024': ctx_1024, 'L0_attn_norm_w': _L0_attn_in['norm_w'], 'L0_attn_Wq': _L0_attn_in['Wq'], 'L0_attn_Wk': _L0_attn_in['Wk'], 'L0_attn_Wv': _L0_attn_in['Wv'], 'L0_attn_Wbeta': _L0_attn_in['Wbeta'], 'L0_attn_bbeta': _L0_attn_in['bbeta'], 'L0_attn_Wig': _L0_attn_in['Wig'], 'L0_attn_big': _L0_attn_in['big'], 'L0_attn_Wog': _L0_attn_in['Wog'], 'L0_attn_bog': _L0_attn_in['bog'], 'L0_attn_Wout': _L0_attn_in['Wout'], 'L0_attn_bout': _L0_attn_in['bout'], 'L0_ffn_gamma': _L0_ffn_in['gamma'], 'L0_ffn_beta': _L0_ffn_in['beta'], 'L0_ffn_gate_w': _L0_ffn_in['gate_w'], 'L0_ffn_w1': _L0_ffn_in['w1'], 'L0_ffn_b1': _L0_ffn_in['b1'], 'L0_ffn_w2': _L0_ffn_in['w2'], 'L0_ffn_b2': _L0_ffn_in['b2']}

def reference(x, ctx_1024, L0_attn_norm_w, L0_attn_Wq, L0_attn_Wk, L0_attn_Wv, L0_attn_Wbeta, L0_attn_bbeta, L0_attn_Wig, L0_attn_big, L0_attn_Wog, L0_attn_bog, L0_attn_Wout, L0_attn_bout, L0_ffn_gamma, L0_ffn_beta, L0_ffn_gate_w, L0_ffn_w1, L0_ffn_b1, L0_ffn_w2, L0_ffn_b2):
    import jax
    import jax.numpy as jnp

    def _L0_attn_ref(x, norm_w, Wq, Wk, Wv, Wbeta, bbeta, Wig, big, Wog, bog, Wout, bout):
        import jax, jax.numpy as jnp
        import numpy as np
        import math
        B, L, HID, NH = (4, 2048, 512, 8)
        DH = HID // NH
        THETA = 10000.0

        def _rope_tables(seq_len, dh):
            half = dh // 2
            inv_freq = 1.0 / THETA ** (jnp.arange(half, dtype=jnp.float32) / half)
            freqs = jnp.arange(seq_len, dtype=jnp.float32)[:, None] * inv_freq[None, :]
            return (jnp.cos(freqs), jnp.sin(freqs))

        def _apply_rope(x, cos, sin):
            half = x.shape[-1] // 2
            x1, x2 = (x[..., :half], x[..., half:2 * half])
            c = cos[None, None]
            s = sin[None, None]
            return jnp.concatenate([x1 * c - x2 * s, x1 * s + x2 * c], axis=-1)
        Bq, Lq, _ = x.shape
        h = x * jax.lax.rsqrt(jnp.mean(x * x, axis=-1, keepdims=True) + 1e-06) * norm_w

        def heads(W):
            return jnp.einsum('bld,ed->ble', h, W).reshape(Bq, Lq, NH, DH).transpose(0, 2, 1, 3)
        q, k, v = (heads(Wq), heads(Wk), heads(Wv))
        cos, sin = _rope_tables(Lq, DH)
        q = _apply_rope(q, cos, sin)
        k = _apply_rope(k, cos, sin)

        def gate(W, b):
            return jax.nn.sigmoid(jnp.einsum('bld,hd->blh', h, W) + b).transpose(0, 2, 1)
        beta, ig, og = (gate(Wbeta, bbeta), gate(Wig, big), gate(Wog, bog))
        scale = 1.0 / math.sqrt(DH)
        qT = q.transpose(2, 0, 1, 3)
        kT = k.transpose(2, 0, 1, 3)
        vT = v.transpose(2, 0, 1, 3)
        fT = beta.transpose(2, 0, 1)
        gT = ig.transpose(2, 0, 1)
        oT = og.transpose(2, 0, 1)
        M0 = jnp.zeros((Bq, NH, DH, DH), x.dtype)

        def step(M, inp):
            q_t, k_t, v_t, f_t, g_t, o_t = inp
            M = M * f_t[..., None, None] + g_t[..., None, None] * scale * (k_t[..., :, None] * v_t[..., None, :])
            y_t = jnp.einsum('bhd,bhde->bhe', q_t, M) * o_t[..., None]
            return (M, y_t)
        _, yT = jax.lax.scan(step, M0, (qT, kT, vT, fT, gT, oT))
        y = yT.transpose(1, 0, 2, 3).reshape(Bq, Lq, HID)
        return jnp.einsum('bld,ed->ble', y, Wout) + bout

    def _L0_xattn_ref(q, k, v):
        import jax, jax.numpy as jnp
        import numpy as np
        DECAY = 0.9
        kv = jnp.swapaxes(k * v, 0, 1)

        def step(r, kv_t):
            r = DECAY * r + kv_t
            return (r, r)
        r0 = jnp.zeros(q.shape[:1] + q.shape[2:], dtype=q.dtype)
        _, rs = jax.lax.scan(step, r0, kv)
        return q * jnp.swapaxes(rs, 0, 1)

    def _L0_ffn_ref(x, gamma, beta, gate_w, w1, b1, w2, b2):
        import jax, jax.numpy as jnp
        import numpy as np
        MICRO_BATCHES = 4
        NUM_EXPERTS = 8
        EPS = 1e-05
        B, S, D = x.shape
        E = w1.shape[0]
        xf = x.reshape(MICRO_BATCHES, -1, D)
        T = xf.shape[1]
        mu = jnp.mean(xf, axis=-1, keepdims=True)
        var = jnp.mean(jnp.square(xf - mu), axis=-1, keepdims=True)
        xn = (xf - mu) * jax.lax.rsqrt(var + EPS) * gamma + beta
        _logits = jnp.einsum('mtd,ed->mte', xn, gate_w)
        _ = jax.lax.top_k(_logits, 2)
        tpe = T // E
        xe = xn.reshape(MICRO_BATCHES, E, tpe, D)
        h = jax.nn.gelu(jnp.einsum('metd,edf->metf', xe, w1) + b1[None, :, None, :], approximate=False)
        y = jnp.einsum('metf,efd->metd', h, w2) + b2[None, :, None, :]
        out = xf + y.reshape(MICRO_BATCHES, T, D)
        return out.reshape(B, S, D)
    x = _layernorm(x + _L0_attn_ref(x, L0_attn_norm_w, L0_attn_Wq, L0_attn_Wk, L0_attn_Wv, L0_attn_Wbeta, L0_attn_bbeta, L0_attn_Wig, L0_attn_big, L0_attn_Wog, L0_attn_bog, L0_attn_Wout, L0_attn_bout), axis=-1)
    x = _layernorm(x + _L0_xattn_ref(x, ctx_1024, ctx_1024), axis=-1)
    x = _layernorm(x + _L0_ffn_ref(x, L0_ffn_gamma, L0_ffn_beta, L0_ffn_gate_w, L0_ffn_w1, L0_ffn_b1, L0_ffn_w2, L0_ffn_b2), axis=-1)
    return x

_drawn_inputs = setup_inputs


def setup_inputs(seed=0):
    import zlib

    import numpy as np

    out = dict(_drawn_inputs(seed))
    spreads = {'L0_attn_norm_w': (1.0, 0.2),
     'L0_attn_bbeta': (2.0, 0.2),
     'L0_attn_big': (0.0, 0.507),
     'L0_attn_bog': (0.0, 0.563),
     'L0_attn_bout': (0.0, 0.1),
     'L0_ffn_gamma': (1.0, 0.2),
     'L0_ffn_beta': (0.0, 0.1),
     'L0_ffn_b1': (0.0, 0.1),
     'L0_ffn_b2': (0.0, 0.1)}
    factors = {}
    for name, (base, spread) in spreads.items():
        noise = np.random.default_rng([zlib.crc32(name.encode()), seed]).standard_normal(out[name].shape)
        drawn = base * np.exp(spread * noise) if base else spread * noise
        out[name] = jnp.asarray(drawn.astype(out[name].dtype))
    for name, factor in factors.items():
        out[name] = (out[name] * factor).astype(out[name].dtype)
    return out
```

```python
from contextlib import ExitStack

import numpy as np

import concourse.bass as bass
from concourse import mybir

F32 = mybir.dt.float32
F32R = mybir.dt.float32r
ALU = mybir.AluOpType
ACT = mybir.ActivationFunctionType

P = 128
B, L, D = 16, 256, 512
NH, DH = 8, 64
HALF = DH // 2
NT = L // P
KC = D // P
E, F = 8, 2048
NM = 4
FC = F // P
SC = 4
CS = FC // SC
SLAB = F // SC
NG = 3 * NH
DW = P + L
GATE_ROW = 32
RMS_EPS, LN_EPS = 1e-6, 1e-5
DECAY, THETA = 0.9, 10000.0


class Step:

    def __init__(self, n, i=None, stride=1):
        self.n, self.i, self.stride = n, i, stride

    def __add__(self, k):
        return Step(self.n + k, self.i, self.stride)

    def __sub__(self, k):
        return self + (-k)

    def within(self, count):
        return 0 <= self.n < count

    def after(self, per, done=0):
        at = self.n * per + done
        return at if self.i is None else self.i * (self.stride * per) + at

    def pair(self, per, done=0):
        at = self.n // 2 * per + done
        return at if self.i is None else self.i * per + at

    @property
    def index(self):
        return self.after(1)

    @property
    def odd(self):
        return self.n % 2


def exact_product(eng, out, lhs_hi, lhs_lo, rhs_hi, rhs_lo, first, last):
    eng.matmul(out, lhs_hi, rhs_hi, start=first, stop=False)
    eng.matmul(out, lhs_hi, rhs_lo, start=False, stop=False)
    return eng.matmul(out, lhs_lo, rhs_hi, start=False, stop=last)


def decoder_layer(nc, x, ctx_in, norm_w, wqT, wkT, wvT, wbetaT, bbeta, wigT, big, wogT, bog,
                  woutT, bout, gamma, beta, w1, b1, w2, b2, rope, decay, out):
    x2_dram = nc.dram_tensor("x2_dram", [B * NT, P, D], F32, kind="Internal").ap()
    with ExitStack() as scope:
        attention_phase(nc, scope, x, ctx_in, norm_w, (wqT, wkT, wvT), (wbetaT, wigT, wogT),
                        (bbeta, big, bog), woutT, bout, rope, decay, x2_dram)
    with ExitStack() as scope:
        expert_phase(nc, scope, x2_dram, gamma, beta, w1, b1, w2, b2, out)


def attention_phase(nc, scope, x, ctx_in, norm_w, wT, wgT, bg, woutT, bout, rope, decay, x2_dram):
    def sb(name, shape, dt=F32):
        return scope.enter_context(nc.sbuf_tensor(name, shape, dt))

    def bank(name, cols=512):
        return scope.enter_context(nc.psum_tensor(name, [P, cols], F32))

    def sem(name):
        return scope.enter_context(nc.semaphore(name))

    wqkv_hi = sb("wqkv_hi", [P, KC, 3 * D], F32R)
    wqkv_lo = sb("wqkv_lo", [P, KC, 3 * D], F32R)
    wg_raw = sb("wg_raw", [P, KC, NG])
    wg_hi = sb("wg_hi", [P, KC, NG], F32R)
    wg_lo = sb("wg_lo", [P, KC, NG], F32R)
    wout_hi = sb("wout_hi", [P, KC, D], F32R)
    wout_lo = sb("wout_lo", [P, KC, D], F32R)
    normw = sb("normw", [P, KC])
    gate_bias = sb("gate_bias", [NG, 1])
    bout_all = sb("bout_all", [P, 1, D])
    rope_sb = sb("rope_sb", [P, NT, 2 * DH])
    decay_sb = sb("decay_sb", [P, 2, P])
    ident = sb("ident_a", [P, P])
    diag = sb("diag", [P, DW])
    head_rows_raw = sb("head_rows_raw", [DH, NH, P])
    head_rows = sb("head_rows", [DH, NH, P], F32R)
    minus_half = sb("minus_half_a", [P, NT])
    rms_eps = sb("rms_eps", [P, NT])
    ln_eps = sb("ln_eps_a", [P, NT])
    zero = sb("zero", [P, 1])
    moment = sb("moment_a", [1, 1])

    x_sb = [sb(f"x{p}", [P, NT, D]) for p in range(2)]
    c_sb = [sb(f"c{p}", [P, NT, D]) for p in range(2)]
    xb = [sb(f"xb{p}", [P, NT, D]) for p in range(2)]
    squares = sb("squares", [P, NT, D])
    sumsq = sb("sumsq", [P, NT])
    rms = sb("rms", [P, NT])
    h = sb("h", [P, NT, D])
    hT_hi = sb("hT_hi", [P, KC, L], F32R)
    hT_lo = sb("hT_lo", [P, KC, L], F32R)
    gates = sb("gates", [NG, DW])
    f_parts = sb("f_parts", [DH, DW], F32R)
    g_tok = sb("g_tok", [P, NT, NH])
    o_tok = sb("o_tok", [P, NT, NH])
    decays = sb("decays", [P, 2, NH, DW])
    rot_a = [sb(f"rot_a{j}", [P, 2 * D]) for j in range(NT)]
    rot_b = [sb(f"rot_b{j}", [P, 2 * D]) for j in range(NT)]
    v_sb = [sb(f"v{p}", [P, NT, D]) for p in range(2)]
    qT = sb("qT", [P, KC, L])
    kT = sb("kT", [P, KC, L])
    probs = sb("probs", [P, 4, DW])
    yT_hi = sb("yT_hi", [P, KC, L], F32R)
    yT_lo = sb("yT_lo", [P, KC, L], F32R)
    res = sb("res", [P, NT, D])
    stats = sb("stats_a", [P, NT, 6])
    mean_var = [sb(f"mean_var{n}", [P, NT, 2]) for n in range(2)]
    rstd = [sb(f"rstd{n}", [P, NT]) for n in range(2)]
    wqkv_raw = decays[:].rearrange("p a h c -> p (a h c)").rearrange("p (k n) -> p k n", k=KC)
    wout_raw = [rot_a[0][:].rearrange("p (k n) -> p k n", n=D), rot_a[1][:].rearrange("p (k n) -> p k n", n=D)]

    turn = [bank(f"turn{n}") for n in range(2)]
    qk_ps = bank("qk_ps", 1024)
    v_ps = bank("v_ps")
    s_ps = [bank(f"s_ps{n}") for n in range(2)]
    spread_ps = bank("spread_ps")
    y_of = [spread_ps, v_ps]

    x_in = [sem(f"x_in{p}") for p in range(2)]
    ctx_loaded = [sem(f"ctx_loaded{p}") for p in range(2)]
    w_in, wout_in, const_in = sem("w_in"), sem("wout_in"), sem("const_in")
    ident_zero, ident_made = sem("ident_zero"), sem("ident_made")
    heads_made, w_hi, w_lo = sem("heads_made"), sem("w_hi"), sem("w_lo")
    fparts_zero = sem("fparts_zero")
    sumsq_done, rms_pre, rms_done = sem("sumsq_done"), sem("rms_pre"), sem("rms_done")
    h_done, xb_done = sem("h_done"), sem("xb_done")
    h_turned, hT_hi_done, hT_lo_done = sem("h_turned"), sem("hT_hi_done"), sem("hT_lo_done")
    gates_ps, gates_done, first_zero = sem("gates_ps"), sem("gates_done"), sem("first_zero")
    f_hi_done, f_lo_done = sem("f_hi_done"), sem("f_lo_done")
    gates_turned, gates_tok = sem("gates_turned"), sem("gates_tok")
    f_spread, decay_done = sem("f_spread"), sem("decay_done")
    v_mm, qk_mm, v_done, rope_done = sem("v_mm"), sem("qk_mm"), sem("v_done"), sem("rope_done")
    rot_done, qo_done = sem("rot_done"), sem("qo_done")
    qk_turned, qkT_done = sem("qk_turned"), sem("qkT_done")
    s_mm, probs_done = sem("s_mm"), sem("probs_done")
    y_mm, y_hi_done, y_lo_done = sem("y_mm"), sem("y_hi_done"), sem("y_lo_done")
    out_mm, res_done, stats_done = sem("out_mm"), sem("res_done"), sem("stats_done")
    mean_done = [sem(f"mean_done{n}") for n in range(2)]
    var_eps = [sem(f"var_eps{n}") for n in range(2)]
    rstd_done = [sem(f"rstd_done{n}") for n in range(2)]
    x1_done, ctx_squared, mem_mm = sem("x1_done"), sem("ctx_squared"), sem("mem_mm")
    u_done, stats2_done, x2_done, x2_stored = sem("u_done"), sem("stats2_done"), sem("x2_done"), sem("x2_stored")

    CONSTS = 8
    first, last = Step(-1), Step(B + 1)

    def steps(eng, body):
        for n in range(-1, 2):
            body(Step(n))
        with eng.Fori(0, (B - 4) // 2) as i:
            for n in (2, 3):
                body(Step(n, i, 2))
        for n in range(B - 2, B + 2):
            body(Step(n))

    with nc.Block() as block:

        @block.sync
        def _(sp):
            def load_x(b):
                if b.n >= 2:
                    sp.wait_ge(h_done, (b - 2).after(NT, NT))
                    sp.wait_ge(xb_done, (b - 2).after(1, 1))
                sp.dma_start(x_sb[b.odd][:], x[b.index].rearrange("(j p) d -> p j d", p=P)).then_inc(x_in[b.odd], 16)

            sp.dma_start(normw[:], norm_w).then_inc(const_in, 16)
            load_x(Step(0))
            for g in range(3):
                sp.dma_start(wg_raw[:, :, g * NH:(g + 1) * NH], wgT[g].rearrange("(k p) n -> p k n", p=P)).then_inc(const_in, 16)
                sp.dma_start(gate_bias[g * NH:(g + 1) * NH, :], bg[g].rearrange("(n a) -> n a", a=1)).then_inc(const_in, 16)
            sp.dma_start(bout_all[:, 0, :], bout.partition_broadcast(P)).then_inc(const_in, 16)
            for n in (2, 0, 1):
                sp.dma_start(wqkv_raw[:, :, n * D:(n + 1) * D], wT[n].rearrange("(k p) n -> p k n", p=P)).then_inc(w_in, 16)
            sp.dma_start(rope_sb[:], rope.rearrange("(j p) c -> p j c", p=P)).then_inc(wout_in, 16)
            sp.dma_start(decay_sb[:], decay.rearrange("p (a c) -> p a c", a=2)).then_inc(wout_in, 16)
            for k in range(NT):
                sp.dma_start(wout_raw[k], woutT[k * 2 * P:(k + 1) * 2 * P, :].rearrange("(k p) n -> p k n", p=P)).then_inc(wout_in, 16)

            def body(b):
                if (b + 2).within(B):
                    load_x(b + 2)
                if b.within(B):
                    if b.n >= 2:
                        sp.wait_ge(mem_mm, (b - 2).after(NT, NT))
                    sp.dma_start(c_sb[b.odd][:], ctx_in[b.index].rearrange("(j p) d -> p j d", p=P)).then_inc(ctx_loaded[b.odd], 16)
                if (b - 2).within(B):
                    sp.wait_ge(x2_done, (b - 2).after(NT, NT))
                    two = (b - 2).index * NT
                    sp.dma_start(x2_dram[bass.ds(two, NT)].rearrange("j p d -> p j d"), res[:]).then_inc(x2_stored, 16)

            load_x(Step(1))
            for n in range(0, 2):
                body(Step(n))
            with sp.Fori(0, (B - 4) // 2) as i:
                for n in (2, 3):
                    body(Step(n, i, 2))
            for n in range(B - 2, B + 2):
                body(Step(n))
            sp.wait_ge(x2_stored, 16 * B)

        @block.scalar
        def _(act):
            act.wait_ge(const_in, 16 * CONSTS)
            for k in range(KC):
                act.activation(wg_hi[:, k, :], wg_raw[:, k, :], ACT.Copy, scale=normw[:, k:k + 1]).then_inc(w_hi, 1)
            act.wait_ge(w_in, 16 * 3)
            for k in range(KC):
                act.activation(wqkv_hi[:, k, :], wqkv_raw[:, k, :], ACT.Copy, scale=normw[:, k:k + 1]).then_inc(w_hi, 1)
            act.wait_ge(wout_in, 16 * (2 + NT))
            for k in range(NT):
                act.activation(wout_hi[:, 2 * k:2 * k + 2, :], wout_raw[k], ACT.Copy).then_inc(w_hi, 1)

            def square_x(b):
                act.wait_ge(x_in[b.odd], b.pair(16, 16))
                if b.n >= 1:
                    act.wait_ge(rms_pre, (b - 1).after(1, 1))
                    act.wait_ge(sumsq_done, (b - 1).after(NT, NT))
                for j in range(NT):
                    act.activation(squares[:, j, :], x_sb[b.odd][:, j, :], ACT.Square,
                                   accum_out=sumsq[:, j:j + 1]).then_inc(sumsq_done, 1)

            def y_high(b):
                for c in range(KC):
                    act.wait_ge(y_mm, b.after(KC, c + 1))
                    if b.n >= 1 and c == 0:
                        act.wait_ge(out_mm, (b - 1).after(NT, NT))
                    act.activation(yT_hi[:, c, :], y_of[c % 2][:, 0:L], ACT.Copy).then_inc(y_hi_done, 1)

            def h_high(b):
                if b.n >= 1:
                    act.wait_ge(qk_mm, (b - 1).after(NT, NT))
                for j in range(NT):
                    act.wait_ge(h_turned, b.after(NT, j + 1))
                    act.activation(hT_hi[:, :, j * P:(j + 1) * P], turn[j][:].rearrange("p (k t) -> p k t", k=KC),
                                   ACT.Copy).then_inc(hT_hi_done, 1)

            def gate(b):
                act.wait_ge(gates_ps, b.after(1, 1))
                if b.n >= 1:
                    act.wait_ge(f_lo_done, (b - 1).after(1, 1))
                    act.wait_ge(gates_turned, (b - 1).after(1, 1))
                act.activation(gates[:, P:DW], v_ps[0:NG, 0:L], ACT.Sigmoid, bias=gate_bias[:]).then_inc(gates_done, 1)
                act.activation(gates[:, 0:P], v_ps[0:NG, P:L], ACT.Sigmoid, bias=gate_bias[:]).then_inc(gates_done, 1)

            def keep_qkT(b):
                if b.n >= 1:
                    act.wait_ge(s_mm, (b - 1).after(NH, NH))
                for j in range(NT):
                    for n, dst in enumerate((qT, kT)):
                        act.wait_ge(qk_turned, b.after(2 * NT, 2 * j + n + 1))
                        act.activation(dst[:, :, j * P:(j + 1) * P], turn[n][:].rearrange("p (k t) -> p k t", k=KC),
                                       ACT.Copy).then_inc(qkT_done, 1)

            def body(b):
                if (b + 1).within(B):
                    square_x(b + 1)
                if (b - 1).within(B):
                    y_high(b - 1)
                if (b + 1).within(B):
                    h_high(b + 1)
                    gate(b + 1)
                if b.within(B):
                    keep_qkT(b)

            steps(act, body)

        @block.gpsimd
        def _(pool):
            pool.memset(ident[:], 0.0).then_inc(ident_zero, 1)
            pool.memset(diag[:], 0.0).then_inc(ident_zero, 1)
            pool.memset(head_rows_raw[:], 0.0).then_inc(ident_zero, 1)
            pool.memset(minus_half[:], -0.5).then_inc(ident_zero, 1)
            pool.memset(zero[:], 0.0).then_inc(ident_zero, 1)
            pool.memset(rms_eps[:], D * RMS_EPS).then_inc(ident_zero, 1)
            pool.memset(ln_eps[:], LN_EPS).then_inc(ident_zero, 1)
            pool.memset(f_parts[:].bitcast(F32), 0.0).then_inc(fparts_zero, 1)
            pool.wait_ge(ident_zero, 7)
            pool.affine_select(out=ident[:], in_=ident[:], compare_op=ALU.not_equal, fill=1.0, base=0,
                               pattern=[[-1, P]], channel_multiplier=1).then_inc(ident_made, 1)
            pool.affine_select(out=diag[:, 0:P], in_=diag[:, 0:P], compare_op=ALU.not_equal, fill=1.0, base=0,
                               pattern=[[-1, P]], channel_multiplier=1).then_inc(ident_made, 1)
            pool.affine_select(out=diag[:, P:DW], in_=diag[:, P:DW], compare_op=ALU.not_equal, fill=1.0, base=0,
                               pattern=[[-1, L]], channel_multiplier=1).then_inc(ident_made, 1)
            pool.affine_select(out=head_rows_raw[:], in_=head_rows_raw[:], compare_op=ALU.not_equal, fill=1.0, base=0,
                               pattern=[[-1, NH], [0, P]], channel_multiplier=1).then_inc(heads_made, 1)
            pool.wait_ge(heads_made, 1)
            pool.affine_select(out=head_rows_raw[:], in_=head_rows_raw[:], compare_op=ALU.not_equal, fill=1.0,
                               base=-GATE_ROW, pattern=[[-1, NH], [0, P]], channel_multiplier=1).then_inc(heads_made, 1)
            pool.wait_ge(const_in, 16 * CONSTS)

            def rms_scale(b):
                pool.wait_ge(sumsq_done, b.after(NT, NT))
                if b.n >= 1:
                    pool.wait_ge(h_done, (b - 1).after(NT, NT))
                pool.tensor_tensor(rms[:], sumsq[:], rms_eps[:], ALU.add).then_inc(rms_pre, 1)
                pool.wait_ge(rms_pre, b.after(1, 1))
                pool.tensor_tensor(rms[:], rms[:], minus_half[:], ALU.pow).then_inc(rms_done, 1)

            def norm_scale(b, n):
                pool.wait_ge(mean_done[n], b.after(NT, NT))
                pool.tensor_tensor(rstd[n][:], mean_var[n][:, :, 1], ln_eps[:], ALU.add).then_inc(var_eps[n], 1)
                pool.wait_ge(var_eps[n], b.after(1, 1))
                pool.tensor_tensor(rstd[n][:], rstd[n][:], minus_half[:], ALU.pow).then_inc(rstd_done[n], 1)

            def square_ctx(b):
                pool.wait_ge(ctx_loaded[b.odd], b.pair(16, 16))
                c = c_sb[b.odd][:]
                pool.tensor_tensor(c, c, c, ALU.mult).then_inc(ctx_squared, 1)

            def rotate(b, j):
                pool.wait_ge(rope_done, b.after(NT, j + 1))
                a = rot_a[j][:]
                pool.tensor_tensor(a, a, rot_b[j][:], ALU.add).then_inc(rot_done, 1)
                pool.wait_ge(rot_done, b.after(NT, j + 1))
                q = rot_a[j][:, 0:D].rearrange("p (h d) -> p h d", h=NH)
                o = o_tok[:, j, :].unsqueeze(2).broadcast_to([P, NH, DH])
                pool.tensor_tensor(q, q, o, ALU.mult).then_inc(qo_done, 1)

            def residual(b):
                pool.wait_ge(x_in[b.odd], b.pair(16, 16))
                if b.n >= 2:
                    pool.wait_ge(res_done, (b - 2).after(NT, NT))
                pool.tensor_tensor(xb[b.odd][:], x_sb[b.odd][:], bout_all[:].broadcast_to([P, NT, D]), ALU.add).then_inc(xb_done, 1)

            def first_column(b):
                pool.wait_ge(gates_done, b.after(2, 2))
                first = gates[0:NH, P:P + 1]
                pool.tensor_tensor(first, first, zero[0:NH, :], ALU.mult).then_inc(first_zero, 1)

            def body(b):
                if (b + 1).within(B):
                    rms_scale(b + 1)
                if (b - 2).within(B):
                    norm_scale(b - 2, 1)
                if (b - 1).within(B):
                    square_ctx(b - 1)
                if b.within(B):
                    rotate(b, 0)
                    rotate(b, 1)
                if (b - 1).within(B):
                    norm_scale(b - 1, 0)
                if (b + 1).within(B):
                    first_column(b + 1)
                    residual(b + 1)

            steps(pool, body)

        @block.vector
        def _(dve):
            dve.wait_ge(heads_made, 2)
            dve.tensor_copy(head_rows[:], head_rows_raw[:]).then_inc(w_lo, 1)
            dve.wait_ge(const_in, 16 * CONSTS)
            for k in range(KC):
                dve.wait_ge(w_hi, k + 1)
                dve.scalar_tensor_tensor(out=wg_lo[:, k, :], in0=wg_raw[:, k, :], scalar=normw[:, k:k + 1],
                                         in1=wg_hi[:, k, :].bitcast(F32), op0=ALU.mult, op1=ALU.subtract).then_inc(w_lo, 1)

            def split_weights():
                dve.wait_ge(w_in, 16 * 3)
                for k in range(KC):
                    dve.wait_ge(w_hi, KC + k + 1)
                    dve.scalar_tensor_tensor(out=wqkv_lo[:, k, :], in0=wqkv_raw[:, k, :], scalar=normw[:, k:k + 1],
                                             in1=wqkv_hi[:, k, :].bitcast(F32), op0=ALU.mult, op1=ALU.subtract).then_inc(w_lo, 1)
                dve.wait_ge(wout_in, 16 * (2 + NT))
                for k in range(NT):
                    dve.wait_ge(w_hi, 2 * KC + k + 1)
                    dve.tensor_tensor(wout_lo[:, 2 * k:2 * k + 2, :], wout_raw[k],
                                      wout_hi[:, 2 * k:2 * k + 2, :].bitcast(F32), ALU.subtract).then_inc(w_lo, 1)
                dve.wait_ge(w_lo, 1 + 2 * KC + NT)

            def scale_h(b):
                dve.wait_ge(rms_done, b.after(1, 1))
                dve.wait_ge(x_in[b.odd], b.pair(16, 16))
                if b.n >= 1:
                    dve.wait_ge(h_turned, (b - 1).after(NT, NT))
                for j in range(NT):
                    dve.tensor_scalar(h[:, j, :], x_sb[b.odd][:, j, :], rms[:, j:j + 1], float(D) ** 0.5,
                                      ALU.mult, ALU.mult).then_inc(h_done, 1)

            def h_low(b):
                for j in range(NT):
                    dve.wait_ge(hT_hi_done, b.after(NT, j + 1))
                    cols = slice(j * P, (j + 1) * P)
                    dve.tensor_tensor(hT_lo[:, :, cols], turn[j][:].rearrange("p (k t) -> p k t", k=KC),
                                      hT_hi[:, :, cols].bitcast(F32), ALU.subtract).then_inc(hT_lo_done, 1)

            def split_gates(b):
                dve.wait_ge(first_zero, b.after(1, 1))
                if b.n >= 1:
                    dve.wait_ge(f_spread, (b - 1).after(NH, NH))
                else:
                    dve.wait_ge(fparts_zero, 1)
                dve.tensor_copy(f_parts[0:NH, :], gates[0:NH, :]).then_inc(f_hi_done, 1)
                dve.wait_ge(f_hi_done, b.after(1, 1))
                dve.tensor_tensor(f_parts[GATE_ROW:GATE_ROW + NH, :], gates[0:NH, :], f_parts[0:NH, :].bitcast(F32),
                                  ALU.subtract).then_inc(f_lo_done, 1)

            def token_gates(b):
                dve.wait_ge(gates_turned, b.after(1, 1))
                if b.n >= 1:
                    dve.wait_ge(v_done, (b - 1).after(NT, NT))
                    dve.wait_ge(qo_done, (b - 1).after(NT, NT))
                tok = v_ps[:, L:L + NT * NG].rearrange("p (j g) -> p j g", g=NG)
                dve.tensor_scalar(g_tok[:], tok[:, :, NH:2 * NH], float(DH) ** -0.5, None, ALU.mult).then_inc(gates_tok, 1)
                dve.tensor_copy(o_tok[:], tok[:, :, 2 * NH:NG]).then_inc(gates_tok, 1)

            def scan(b, n):
                dve.wait_ge(f_spread, b.after(NH, n + 1))
                if b.n >= 2 and n == 0:
                    dve.wait_ge(probs_done, (b - 2).after(NH, NH))
                dve.tensor_tensor_scan(decays[:, b.odd, n, :], spread_ps[:, 0:DW], diag[:], 0.0, ALU.mult, ALU.add).then_inc(decay_done, 1)

            def gate_v(b, j):
                dve.wait_ge(v_mm, b.after(NT, j + 1))
                dve.wait_ge(gates_tok, b.after(2, 2))
                if b.n >= 2 and j == 0:
                    dve.wait_ge(y_mm, (b - 2).after(KC, KC))
                dve.tensor_tensor(v_sb[b.odd][:, j, :].rearrange("p (h d) -> p h d", h=NH),
                                  v_ps[:].rearrange("p (h d) -> p h d", h=NH),
                                  g_tok[:, j, :].unsqueeze(2).broadcast_to([P, NH, DH]), ALU.mult).then_inc(v_done, 1)

            def rope_parts(b, j):
                dve.wait_ge(qk_mm, b.after(NT, j + 1))
                if b.n >= 1:
                    dve.wait_ge(qk_turned, (b - 1).after(2 * NT, 2 * NT))
                src = qk_ps[:].rearrange("p (h d) -> p h d", d=DH)
                a = rot_a[j][:].rearrange("p (h d) -> p h d", d=DH)
                s = rot_b[j][:].rearrange("p (h d) -> p h d", d=DH)

                def table(lo, hi):
                    return rope_sb[:, j:j + 1, lo:hi].broadcast_to([P, 2 * NH, hi - lo])

                dve.tensor_tensor(a, src, table(0, DH), ALU.mult)
                dve.tensor_tensor(s[:, :, 0:HALF], src[:, :, HALF:DH], table(DH, DH + HALF), ALU.mult)
                dve.tensor_tensor(s[:, :, HALF:DH], src[:, :, 0:HALF], table(DH + HALF, 2 * DH), ALU.mult).then_inc(rope_done, 1)

            def weigh(b, n):
                dve.wait_ge(s_mm, b.after(NH, n + 1))
                dve.wait_ge(decay_done, b.after(NH, n + 1))
                if n >= 4:
                    dve.wait_ge(y_mm, b.after(KC, (n - 4) // 2 + 1))
                elif b.n >= 1:
                    dve.wait_ge(y_mm, (b - 1).after(KC, (n + 4) // 2 + 1))
                dve.tensor_tensor(probs[:, n % 4, :], s_ps[n % 2][:, 0:DW], decays[:, b.odd, n, :], ALU.mult).then_inc(probs_done, 1)

            def y_low(b, c):
                dve.wait_ge(y_hi_done, b.after(KC, c + 1))
                dve.tensor_tensor(yT_lo[:, c, :], y_of[c % 2][:, 0:L], yT_hi[:, c, :].bitcast(F32),
                                  ALU.subtract).then_inc(y_lo_done, 1)

            def add_residual(b):
                if b.n >= 1:
                    dve.wait_ge(x2_stored, (b - 1).after(16, 16))
                dve.wait_ge(xb_done, b.after(1, 1))
                for j in range(NT):
                    dve.wait_ge(out_mm, b.after(NT, j + 1))
                    dve.tensor_tensor(res[:, j, :], s_ps[j][:], xb[b.odd][:, j, :], ALU.add).then_inc(res_done, 1)

            def norm_stats(b, n):
                made, seen = ((res_done, stats_done), (u_done, stats2_done))[n]
                for j in range(NT):
                    dve.wait_ge(made, b.after(NT, j + 1))
                    dve.bn_stats(stats[:, j, :], res[:, j, :]).then_inc(seen, 1)
                dve.wait_ge(seen, b.after(NT, NT))
                dve.memset(moment[:], 0.0)
                for j in range(NT):
                    dve.bn_aggr(mean_var[n][:, j, :], stats[:, j, :]).then_inc(mean_done[n], 1)

            def normalize(b, n):
                dve.wait_ge(rstd_done[n], b.after(1, 1))
                for j in range(NT):
                    dve.tensor_scalar(res[:, j, :], res[:, j, :], mean_var[n][:, j, 0:1], rstd[n][:, j:j + 1],
                                      ALU.subtract, ALU.mult).then_inc((x1_done, x2_done)[n], 1)

            def add_memory(b):
                for j in range(NT):
                    dve.wait_ge(mem_mm, b.after(NT, j + 1))
                    dve.wait_ge(x1_done, b.after(NT, j + 1))
                    dve.scalar_tensor_tensor(out=res[:, j, :], in0=qk_ps[:, j * D:(j + 1) * D], scalar=1.0,
                                             in1=res[:, j, :], op0=ALU.add, op1=ALU.mult).then_inc(u_done, 1)

            def body(b):
                if (b - 2).within(B):
                    add_memory(b - 2)
                    norm_stats(b - 2, 1)
                if b.within(B):
                    scan(b, 0)
                    gate_v(b, 0)
                if (b - 2).within(B):
                    normalize(b - 2, 1)
                if b.within(B):
                    for n in (1, 2, 3):
                        scan(b, n)
                    rope_parts(b, 0)
                    scan(b, 4)
                    gate_v(b, 1)
                    for n in (5, 6, 7):
                        scan(b, n)
                    rope_parts(b, 1)
                if (b + 1).within(B):
                    scale_h(b + 1)
                if (b - 1).within(B):
                    for n in range(NH):
                        weigh(b - 1, n)
                        if n in (3, 5, 7):
                            y_low(b - 1, (n - 3) // 2)
                    y_low(b - 1, KC - 1)
                if (b + 1).within(B):
                    h_low(b + 1)
                if (b - 1).within(B):
                    add_residual(b - 1)
                    norm_stats(b - 1, 0)
                if (b + 1).within(B):
                    split_gates(b + 1)
                if (b - 1).within(B):
                    normalize(b - 1, 0)
                if (b + 1).within(B):
                    token_gates(b + 1)
                if b.n == -1:
                    split_weights()

            steps(dve, body)

        @block.tensor
        def _(pe):
            def turn_h(b):
                if b.n >= 2:
                    pe.wait_ge(qkT_done, (b - 2).after(2 * NT, 2 * NT))
                else:
                    pe.wait_ge(ident_made, 3)
                for j in range(NT):
                    pe.wait_ge(h_done, b.after(NT, j + 1))
                    for k in range(KC):
                        mm = pe.transpose(turn[j][:, k * P:(k + 1) * P], h[:, j, k * P:(k + 1) * P], ident[:])
                    mm.then_inc(h_turned, 1)

            def gate_products(b):
                if b.n == 0:
                    pe.wait_ge(w_lo, 1 + KC)
                else:
                    pe.wait_ge(v_done, (b - 1).after(NT, NT))
                pe.wait_ge(hT_lo_done, b.after(NT, NT))
                for k in range(KC):
                    mm = exact_product(pe, v_ps[0:NG, 0:L], wg_hi[:, k, :], wg_lo[:, k, :],
                                       hT_hi[:, k, :], hT_lo[:, k, :], k == 0, k == KC - 1)
                mm.then_inc(gates_ps, 1)

            def turn_gates(b):
                pe.wait_ge(first_zero, b.after(1, 1))
                for j in range(NT):
                    mm = pe.matmul(v_ps[:, L + j * NG:L + (j + 1) * NG], gates[:, (j + 1) * P:(j + 2) * P],
                                   ident[0:NG, 0:NG], start=True, stop=True)
                mm.then_inc(gates_turned, 1)

            def spread_f(b, n):
                if n == 0:
                    pe.wait_ge(f_lo_done, b.after(1, 1))
                    if b.n >= 2:
                        pe.wait_ge(y_lo_done, (b - 2).after(KC, KC))
                else:
                    pe.wait_ge(decay_done, b.after(NH, n))
                pe.matmul(spread_ps[:, 0:DW], head_rows[:, n, :], f_parts[:], start=True, stop=True).then_inc(f_spread, 1)

            def project(b):
                spreads = iter(range(NH))
                groups = 0
                for j in range(NT):
                    for n, dst in ((2, v_ps[:]), (0, qk_ps[:, 0:D]), (1, qk_ps[:, D:2 * D])):
                        if n == 2 and j == 0:
                            pe.wait_ge(gates_tok, b.after(2, 2))
                        elif n == 2:
                            pe.wait_ge(v_done, b.after(NT, 1))
                        elif n == 0 and j == 0 and b.n >= 2:
                            pe.wait_ge(u_done, (b - 2).after(NT, NT))
                        elif n == 0 and j == 1:
                            pe.wait_ge(rope_done, b.after(NT, 1))
                        for k in range(KC):
                            tok = slice(j * P, (j + 1) * P)
                            mm = exact_product(pe, dst, hT_hi[:, k, tok], hT_lo[:, k, tok],
                                               wqkv_hi[:, k, n * D:(n + 1) * D], wqkv_lo[:, k, n * D:(n + 1) * D],
                                               k == 0, k == KC - 1)
                            if k == KC - 1 and n == 2:
                                mm.then_inc(v_mm, 1)
                            if k == KC - 1 and n == 1:
                                mm.then_inc(qk_mm, 1)
                            groups += 1
                            if groups % 3 == 0:
                                spread_f(b, next(spreads))

            def turn_qk(b):
                for j in range(NT):
                    pe.wait_ge(qo_done, b.after(NT, j + 1))
                    for n in range(2):
                        if j == 1:
                            pe.wait_ge(qkT_done, b.after(2 * NT, n + 1))
                        elif (b + 1).within(B):
                            pe.wait_ge(hT_lo_done, (b + 1).after(NT, NT))
                        for k in range(KC):
                            mm = pe.transpose(turn[n][:, k * P:(k + 1) * P],
                                              rot_a[j][:, n * D + k * P:n * D + (k + 1) * P], ident[:])
                        mm.then_inc(qk_turned, 1)

            def scores(b, n):
                rows, c = slice(n % 2 * DH, (n % 2 + 1) * DH), n // 2
                if n == 0:
                    pe.wait_ge(qkT_done, b.after(2 * NT, 2 * NT))
                if n >= 2:
                    pe.wait_ge(probs_done, b.after(NH, n - 1))
                elif b.n >= 1:
                    pe.wait_ge(res_done, (b - 1).after(NT, n + 1))
                s = s_ps[n % 2]
                pe.matmul(s[:, 0:P], kT[rows, c, P:L], qT[rows, c, P:L], start=True, stop=True)
                pe.matmul(s[:, P:DW], kT[rows, c, 0:P], qT[rows, c, 0:L], start=True, stop=True).then_inc(s_mm, 1)

            def weighted_values(b, c):
                if c == 0 and (b + 1).within(B):
                    pe.wait_ge(decay_done, (b + 1).after(NH, NH))
                if c == 1 and (b + 1).within(B):
                    pe.wait_ge(v_done, (b + 1).after(NT, NT))
                if c >= 2:
                    pe.wait_ge(y_lo_done, b.after(KC, c - 1))
                v = v_sb[b.odd]
                pe.wait_ge(probs_done, b.after(NH, 2 * c + 2))
                for n in (2 * c, 2 * c + 1):
                    rows = slice(n % 2 * DH, (n % 2 + 1) * DH)
                    pe.matmul(y_of[c % 2][rows, 0:L], v[:, 0, n * DH:(n + 1) * DH], probs[:, n % 4, P:DW],
                              start=True, stop=False)
                for n in (2 * c, 2 * c + 1):
                    rows = slice(n % 2 * DH, (n % 2 + 1) * DH)
                    mm = pe.matmul(y_of[c % 2][rows, P:L], v[:, 1, n * DH:(n + 1) * DH], probs[:, n % 4, 0:P],
                                   start=False, stop=True)
                mm.then_inc(y_mm, 1)

            def attend(b):
                for n in range(NH):
                    scores(b, n)
                    if n in (3, 5, 7):
                        weighted_values(b, (n - 3) // 2)
                weighted_values(b, KC - 1)

            def project_out(b):
                for j in range(NT):
                    pe.wait_ge(probs_done, b.after(NH, NH))
                    for k in range(KC):
                        if j == 0:
                            pe.wait_ge(y_lo_done, b.after(KC, k + 1))
                        tok = slice(j * P, (j + 1) * P)
                        mm = exact_product(pe, s_ps[j][:], yT_hi[:, k, tok], yT_lo[:, k, tok],
                                           wout_hi[:, k, :], wout_lo[:, k, :], k == 0, k == KC - 1)
                    mm.then_inc(out_mm, 1)

            def cross_memory(b):
                pe.wait_ge(ctx_squared, b.after(1, 1))
                if (b + 1).within(B):
                    pe.wait_ge(rope_done, (b + 1).after(NT, NT))
                c = c_sb[b.odd]
                pe.matmul(qk_ps[:, 0:D], decay_sb[:, 0, :], c[:, 0, :], start=True, stop=True).then_inc(mem_mm, 1)
                pe.matmul(qk_ps[:, D:2 * D], decay_sb[:, 1, :], c[:, 0, :], start=True, stop=False)
                pe.matmul(qk_ps[:, D:2 * D], decay_sb[:, 0, :], c[:, 1, :], start=False, stop=True).then_inc(mem_mm, 1)

            def body(b):
                if b.within(B):
                    if b.n == 0:
                        pe.wait_ge(w_lo, 1 + 2 * KC + NT)
                    project(b)
                if (b - 1).within(B):
                    attend(b - 1)
                if (b + 1).within(B):
                    turn_h(b + 1)
                if (b - 1).within(B):
                    project_out(b - 1)
                if (b + 1).within(B):
                    gate_products(b + 1)
                if b.within(B):
                    turn_qk(b)
                if (b - 1).within(B):
                    cross_memory(b - 1)
                if (b + 1).within(B):
                    turn_gates(b + 1)

            steps(pe, body)


def expert_phase(nc, scope, x2_dram, gamma, beta, w1, b1, w2, b2, out):
    def sb(name, shape, dt=F32):
        return scope.enter_context(nc.sbuf_tensor(name, shape, dt))

    def bank(name):
        return scope.enter_context(nc.psum_tensor(name, [P, 512], F32))

    def sem(name):
        return scope.enter_context(nc.semaphore(name))

    x2_view = x2_dram.rearrange("(m t) p d -> t p m d", t=E)
    out_view = out.rearrange("b (j p) d -> (b j) p d", p=P).rearrange("(m t) p d -> t p m d", t=E)
    T = NM * P

    ident = sb("ident_b", [P, P])
    minus_half = sb("minus_half_b", [P, NM])
    ln_eps = sb("ln_eps_b", [P, NM])
    moment = sb("moment_b", [1, 1])
    gamma_sb = sb("gamma_sb", [P, KC])
    beta_sb = sb("beta_sb", [P, KC])
    b1_cols = sb("b1_cols", [P, E * FC])
    w1_raw = [sb(f"w1_raw{s}", [P, KC, SLAB]) for s in range(2)]
    w2_raw = [sb(f"w2_raw{s}", [P, CS, D]) for s in range(2)]
    w1_hi = [sb(f"w1_hi{s}", [P, KC, SLAB], F32R) for s in range(2)]
    w1_lo = [sb(f"w1_lo{s}", [P, KC, SLAB], F32R) for s in range(2)]
    w2_hi = [sb(f"w2_hi{s}", [P, CS, D], F32R) for s in range(2)]
    w2_lo = [sb(f"w2_lo{s}", [P, CS, D], F32R) for s in range(2)]
    x2 = sb("x2", [P, NM, D])
    x2b = sb("x2b", [P, NM, D])
    b2_all = sb("b2_all", [P, 1, D])
    xn = sb("xn", [P, NM, D])
    xnT = sb("xnT", [P, KC, T])
    xnT_hi = sb("xnT_hi", [P, KC, T], F32R)
    xnT_lo = sb("xnT_lo", [P, KC, T], F32R)
    hid = [sb(f"hid{n}", [P, T]) for n in range(2)]
    hid_hi = [sb(f"hid_hi{n}", [P, T], F32R) for n in range(2)]
    hid_lo = [sb(f"hid_lo{n}", [P, T], F32R) for n in range(2)]
    res = sb("res_b", [P, NM, D])
    stats = [sb(f"stats_b{n}", [P, NM, 6]) for n in range(2)]
    mean_var = [sb(f"mean_var_b{n}", [P, NM, 2]) for n in range(2)]
    rstd = [sb(f"rstd_b{n}", [P, NM]) for n in range(2)]

    acc = [bank(f"acc{m}") for m in range(NM)]
    up_ps = [bank(f"up{n}") for n in range(2)]
    turn = [bank(f"turn_b{n}") for n in range(2)]

    const_in, ident_made, ident_zero = sem("const_in_b"), sem("ident_made_b"), sem("ident_zero_b")
    w1_in = [sem(f"w1_in{s}") for s in range(2)]
    w2_in = [sem(f"w2_in{s}") for s in range(2)]
    w1_hi_done, w1_lo_done = sem("w1_hi_done"), sem("w1_lo_done")
    w2_hi_done, w2_lo_done = sem("w2_hi_done"), sem("w2_lo_done")
    x2_in, b2_in, x2b_done = sem("x2_in"), sem("b2_in"), sem("x2b_done")
    x2b_half = sem("x2b_half")
    stats_done = [sem(f"stats_done_b{n}") for n in range(2)]
    mean_done = [sem(f"mean_done_b{n}") for n in range(2)]
    var_eps = [sem(f"var_eps_b{n}") for n in range(2)]
    rstd_done = [sem(f"rstd_done_b{n}") for n in range(2)]
    xn_done, xn_turned, xnT_done = sem("xn_done"), sem("xn_turned"), sem("xnT_done")
    xnT_hi_done, xnT_lo_done = sem("xnT_hi_done"), sem("xnT_lo_done")
    up_mm, down_mm, gelu_done = sem("up_mm"), sem("down_mm"), sem("gelu_done")
    hid_hi_done, hid_lo_done = sem("hid_hi_done"), sem("hid_lo_done")
    res_done, out_done, out_stored = sem("res_done_b"), sem("out_done"), sem("out_stored")

    def experts(eng, body):
        with eng.Fori(0, E - 1) as i:
            body(Step(0, i), True)
        body(Step(E - 1), False)

    def slab(e, s):
        return (e + s // SC), s % SC

    with nc.Block() as block:

        @block.sync
        def _(sp):
            def load_slab(e, s):
                e, s = slab(e, s)
                if not (e.i is None and e.n == 0 and s < 2):
                    sp.wait_ge(w1_lo_done, e.after(SC, s - 1))
                    sp.wait_ge(w2_lo_done, e.after(SC, s - 1))
                    sp.wait_ge(w1_hi_done, e.after(SC, s - 1))
                    sp.wait_ge(w2_hi_done, e.after(SC, s - 1))
                sp.dma_start(w1_raw[s % 2][:], w1[e.index].rearrange("(k p) f -> p k f", p=P)[:, :, s * SLAB:(s + 1) * SLAB])\
                    .then_inc(w1_in[s % 2], 16)
                sp.dma_start(w2_raw[s % 2][:], w2[e.index].rearrange("(s c p) d -> s p c d", p=P, c=CS)[s])\
                    .then_inc(w2_in[s % 2], 16)

            def load_tokens(e):
                sp.dma_start(x2[:], x2_view[e.index]).then_inc(x2_in, 16)
                sp.dma_start(b2_all[:, 0, :], b2[e.index].partition_broadcast(P)).then_inc(b2_in, 16)

            load_tokens(Step(0))
            sp.dma_start(gamma_sb[:], gamma).then_inc(const_in, 16)
            sp.dma_start(beta_sb[:], beta).then_inc(const_in, 16)
            sp.dma_start(b1_cols[:], b1).then_inc(const_in, 16)
            load_slab(Step(0), 0)
            load_slab(Step(0), 1)

            def store(e):
                sp.wait_ge(out_done, e.after(NM, NM))
                sp.dma_start(out_view[e.index], res[:]).then_inc(out_stored, 16)

            def body(e, more):
                load_slab(e, 2)
                if more:
                    sp.wait_ge(x2b_done, e.after(1, 1))
                    load_tokens(e + 1)
                load_slab(e, 3)
                if more:
                    load_slab(e, 4)
                    load_slab(e, 5)
                store(e)

            experts(sp, body)
            sp.wait_ge(out_stored, 16 * E)

        @block.scalar
        def _(act):
            def split_w1(e, s):
                e, s = slab(e, s)
                act.wait_ge(w1_in[s % 2], e.after(16 * SC // 2, 16 * (s // 2 + 1)))
                if not (e.i is None and e.n == 0 and s < 2):
                    act.wait_ge(up_mm, e.after(FC, CS * (s - 1)))
                act.activation(w1_hi[s % 2][:], w1_raw[s % 2][:], ACT.Copy).then_inc(w1_hi_done, 1)

            def split_w2(e, s):
                e, s = slab(e, s)
                act.wait_ge(w2_in[s % 2], e.after(16 * SC // 2, 16 * (s // 2 + 1)))
                if not (e.i is None and e.n == 0 and s < 2):
                    act.wait_ge(down_mm, e.after(FC, CS * (s - 1)))
                act.activation(w2_hi[s % 2][:], w2_raw[s % 2][:], ACT.Copy).then_inc(w2_hi_done, 1)

            def split_tokens(e):
                for k in range(KC):
                    act.wait_ge(xnT_done, e.after(KC, k + 1))
                    if k == 0 and not (e.i is None and e.n == 0):
                        act.wait_ge(up_mm, e.after(FC, 0))
                    act.activation(xnT_hi[:, k, :], xnT[:, k, :], ACT.Copy).then_inc(xnT_hi_done, 1)

            def gelu(e, c):
                act.wait_ge(up_mm, e.after(FC, c + 1))
                if c >= 2 or not (e.i is None and e.n == 0):
                    act.wait_ge(hid_lo_done, e.after(FC, c - 1))
                act.activation(hid[c % 2][:], up_ps[c % 2][:], ACT.Gelu,
                               bias=b1_cols[:, bass.ds(e.after(FC, c), 1)]).then_inc(gelu_done, 1)

            split_w1(Step(0), 0)
            split_w2(Step(0), 0)
            act.wait_ge(const_in, 16 * 3)
            split_tokens(Step(0))

            def body(e, more):
                for c in range(FC):
                    if c == FC - 1 and more:
                        split_tokens(e + 1)
                    gelu(e, c)
                    if c % CS == 0 and (more or c // CS + 1 < SC):
                        split_w1(e, c // CS + 1)
                    if c % CS == 1 and (more or c // CS + 1 < SC):
                        split_w2(e, c // CS + 1)

            def peeled(e, more):
                body(e, more)

            body(Step(0), True)
            with act.Fori(0, E - 2) as i:
                body(Step(1, i), True)
            peeled(Step(E - 1), False)

        @block.gpsimd
        def _(pool):
            pool.memset(ident[:], 0.0).then_inc(ident_zero, 1)
            pool.memset(minus_half[:], -0.5).then_inc(ident_zero, 1)
            pool.memset(ln_eps[:], LN_EPS).then_inc(ident_zero, 1)
            pool.wait_ge(ident_zero, 3)
            pool.affine_select(out=ident[:], in_=ident[:], compare_op=ALU.not_equal, fill=1.0, base=0,
                               pattern=[[-1, P]], channel_multiplier=1).then_inc(ident_made, 1)

            def norm_scale(e, n):
                pool.wait_ge(mean_done[n], e.after(NM, NM))
                pool.tensor_tensor(rstd[n][:], mean_var[n][:, :, 1], ln_eps[:], ALU.add).then_inc(var_eps[n], 1)
                pool.wait_ge(var_eps[n], e.after(1, 1))
                pool.tensor_tensor(rstd[n][:], rstd[n][:], minus_half[:], ALU.pow).then_inc(rstd_done[n], 1)

            def add_b2(e):
                pool.wait_ge(x2_in, e.after(16, 16))
                pool.wait_ge(b2_in, e.after(16, 16))
                pool.wait_ge(xn_done, e.after(NM, NM))
                if e.n >= 1:
                    pool.wait_ge(res_done, e.after(NM, 0))
                pool.tensor_tensor(x2b[:], x2[:], b2_all[:].broadcast_to([P, NM, D]), ALU.add).then_inc(x2b_half, 1)
                pool.wait_ge(x2b_half, e.after(1, 1))
                pool.tensor_tensor(x2b[:], x2b[:], x2[:], ALU.add).then_inc(x2b_done, 1)

            def split_w2(e, s):
                e, s = slab(e, s)
                pool.wait_ge(w2_hi_done, e.after(SC, s + 1))
                pool.tensor_tensor(w2_lo[s % 2][:], w2_raw[s % 2][:], w2_hi[s % 2][:].bitcast(F32), ALU.subtract)\
                    .then_inc(w2_lo_done, 1)

            norm_scale(Step(0), 0)
            split_w2(Step(0), 0)

            def body(e, more):
                if e.n >= 1:
                    norm_scale(e - 1, 1)
                add_b2(e)
                for s in range(SC):
                    if more or s + 1 < SC:
                        split_w2(e, s + 1)
                    if s == 1 and more:
                        norm_scale(e + 1, 0)

            body(Step(0), True)
            with pool.Fori(0, E - 2) as i:
                body(Step(1, i), True)
            body(Step(E - 1), False)
            norm_scale(Step(E - 1), 1)

        @block.vector
        def _(dve):
            def norm_stats(e, n):
                src = (x2, res)[n]
                if n == 0:
                    dve.wait_ge(x2_in, e.after(16, 16))
                for m in range(NM):
                    if n == 1:
                        dve.wait_ge(res_done, e.after(NM, m + 1))
                    dve.bn_stats(stats[n][:, m, :], src[:, m, :]).then_inc(stats_done[n], 1)
                dve.wait_ge(stats_done[n], e.after(NM, NM))
                dve.memset(moment[:], 0.0)
                for m in range(NM):
                    dve.bn_aggr(mean_var[n][:, m, :], stats[n][:, m, :]).then_inc(mean_done[n], 1)

            def normalize(e, n):
                src, dst = ((x2, xn), (res, res))[n]
                dve.wait_ge(rstd_done[n], e.after(1, 1))
                if n == 0 and e.n >= 1:
                    dve.wait_ge(xn_turned, e.after(KC, 0))
                for m in range(NM):
                    dve.tensor_scalar(dst[:, m, :], src[:, m, :], mean_var[n][:, m, 0:1], rstd[n][:, m:m + 1],
                                      ALU.subtract, ALU.mult).then_inc((xn_done, out_done)[n], 1)

            def affine(e, k):
                dve.wait_ge(xn_turned, e.after(KC, k + 1))
                if e.n >= 1 and k == 0:
                    dve.wait_ge(xnT_hi_done, e.after(KC, 0))
                    dve.wait_ge(xnT_lo_done, e.after(KC, 0))
                dve.tensor_scalar(xnT[:, k, :], turn[k % 2][:], gamma_sb[:, k:k + 1], beta_sb[:, k:k + 1],
                                  ALU.mult, ALU.add).then_inc(xnT_done, 1)

            def tokens_low(e):
                for k in range(KC):
                    dve.wait_ge(xnT_hi_done, e.after(KC, k + 1))
                    dve.tensor_tensor(xnT_lo[:, k, :], xnT[:, k, :], xnT_hi[:, k, :].bitcast(F32), ALU.subtract)\
                        .then_inc(xnT_lo_done, 1)

            def split_w1(e, s):
                e, s = slab(e, s)
                dve.wait_ge(w1_hi_done, e.after(SC, s + 1))
                dve.tensor_tensor(w1_lo[s % 2][:], w1_raw[s % 2][:], w1_hi[s % 2][:].bitcast(F32), ALU.subtract)\
                    .then_inc(w1_lo_done, 1)

            def split_hidden(e, c):
                dve.wait_ge(gelu_done, e.after(FC, c + 1))
                if c >= 2 or e.n >= 1:
                    dve.wait_ge(down_mm, e.after(FC, c - 1))
                dve.tensor_copy(hid_hi[c % 2][:], hid[c % 2][:]).then_inc(hid_hi_done, 1)
                dve.wait_ge(hid_hi_done, e.after(FC, c + 1))
                dve.tensor_tensor(hid_lo[c % 2][:], hid[c % 2][:], hid_hi[c % 2][:].bitcast(F32), ALU.subtract)\
                    .then_inc(hid_lo_done, 1)

            def add_residual(e):
                dve.wait_ge(down_mm, e.after(FC, FC))
                dve.wait_ge(x2b_done, e.after(1, 1))
                if e.n >= 1:
                    dve.wait_ge(out_stored, e.after(16, 0))
                for m in range(NM):
                    dve.tensor_tensor(res[:, m, :], acc[m][:], x2b[:, m, :], ALU.add).then_inc(res_done, 1)

            norm_stats(Step(0), 0)
            split_w1(Step(0), 0)
            normalize(Step(0), 0)
            dve.wait_ge(const_in, 16 * 3)
            for k in range(KC):
                affine(Step(0), k)
            tokens_low(Step(0))

            def body(e, more):
                for c in range(FC):
                    if c == FC - 1 and more:
                        tokens_low(e + 1)
                    split_hidden(e, c)
                    if e.n >= 1:
                        if c == 0:
                            add_residual(e - 1)
                        if c == 1:
                            norm_stats(e - 1, 1)
                        if c == 3:
                            normalize(e - 1, 1)
                    if c % CS == 2 and (more or c // CS + 1 < SC):
                        split_w1(e, c // CS + 1)
                    if more:
                        if c == 8:
                            norm_stats(e + 1, 0)
                        if c == 9:
                            normalize(e + 1, 0)
                        if 11 <= c < 11 + KC:
                            affine(e + 1, c - 11)

            body(Step(0), True)
            body(Step(1), True)
            with dve.Fori(0, E - 3) as i:
                body(Step(2, i), True)
            body(Step(E - 1), False)
            add_residual(Step(E - 1))
            norm_stats(Step(E - 1), 1)
            normalize(Step(E - 1), 1)

        @block.tensor
        def _(pe):
            def turn_tokens(e, k):
                if k == 0:
                    pe.wait_ge(xn_done, e.after(NM, NM))
                if k >= 2 or e.n >= 1:
                    pe.wait_ge(xnT_done, e.after(KC, k - 1))
                for m in range(NM):
                    mm = pe.transpose(turn[k % 2][:, m * P:(m + 1) * P], xn[:, m, k * P:(k + 1) * P], ident[:])
                mm.then_inc(xn_turned, 1)

            def up(e, c):
                s = c // CS
                if c % CS == 0:
                    pe.wait_ge(w1_lo_done, e.after(SC, s + 1))
                if c >= 2 or e.n >= 1:
                    pe.wait_ge(gelu_done, e.after(FC, c - 1))
                cols = slice(c % CS * P, (c % CS + 1) * P)
                for k in range(KC):
                    if c == 0:
                        pe.wait_ge(xnT_lo_done, e.after(KC, k + 1))
                    mm = exact_product(pe, up_ps[c % 2][:], w1_hi[s % 2][:, k, cols], w1_lo[s % 2][:, k, cols],
                                       xnT_hi[:, k, :], xnT_lo[:, k, :], k == 0, k == KC - 1)
                mm.then_inc(up_mm, 1)

            def down(e, c):
                s = c // CS
                if c % CS == 0:
                    pe.wait_ge(w2_lo_done, e.after(SC, s + 1))
                pe.wait_ge(hid_lo_done, e.after(FC, c + 1))
                for m in range(NM):
                    if c == 0 and (e.n >= 1):
                        pe.wait_ge(res_done, e.after(NM, m + 1 - NM))
                    tok = slice(m * P, (m + 1) * P)
                    mm = exact_product(pe, acc[m][:], hid_hi[c % 2][:, tok], hid_lo[c % 2][:, tok],
                                       w2_hi[s % 2][:, c % CS, :], w2_lo[s % 2][:, c % CS, :], c == 0, c == FC - 1)
                mm.then_inc(down_mm, 1)

            pe.wait_ge(ident_made, 1)
            for k in range(KC):
                turn_tokens(Step(0), k)
            up(Step(0), 0)

            def body(e, more):
                for c in range(1, FC):
                    up(e, c)
                    down(e, c - 1)
                    if more and 11 <= c < 11 + KC:
                        turn_tokens(e + 1, c - 11)
                if more:
                    up(e + 1, 0)
                down(e, FC - 1)

            body(Step(0), True)
            with pe.Fori(0, E - 2) as i:
                body(Step(1, i), True)
            body(Step(E - 1), False)


def rope_tables():
    half = np.arange(HALF, dtype=np.float32) / np.float32(HALF)
    inv_freq = np.float32(1.0) / np.float32(THETA) ** half
    angles = np.arange(L, dtype=np.float32)[:, None] * inv_freq[None, :]
    cos, sin = np.cos(angles), np.sin(angles)
    return np.ascontiguousarray(np.concatenate([cos, cos, -sin, sin], axis=1), np.float32)


def decay_tables():
    step = np.arange(P)[None, :] - np.arange(P)[:, None]
    base = float(np.float32(DECAY))
    within = np.where(step >= 0, base ** np.maximum(step, 0), 0.0)
    return np.ascontiguousarray(np.concatenate([within, base ** (step + P)], axis=1), np.float32)


def kernel(**inputs):
    import concourse.bacc as _bacc
    from concourse.bass_utils import run_bass_kernel_spmd as _run

    def arr(name):
        return np.ascontiguousarray(inputs[name])

    def turned(name):
        return np.ascontiguousarray(np.asarray(inputs[name]).T)

    def columns(name):
        return np.ascontiguousarray(np.asarray(inputs[name]).reshape(-1, P).T)

    a = "L0_attn_"
    f = "L0_ffn_"
    arrays = {
        "x": arr("x"), "ctx_in": arr("ctx_1024"), "norm_w": columns(a + "norm_w"),
        "wqT": turned(a + "Wq"), "wkT": turned(a + "Wk"), "wvT": turned(a + "Wv"),
        "wbetaT": turned(a + "Wbeta"), "bbeta": arr(a + "bbeta"), "wigT": turned(a + "Wig"), "big": arr(a + "big"),
        "wogT": turned(a + "Wog"), "bog": arr(a + "bog"), "woutT": turned(a + "Wout"), "bout": arr(a + "bout"),
        "gamma": columns(f + "gamma"), "beta": columns(f + "beta"), "w1": arr(f + "w1"), "b1": columns(f + "b1"),
        "w2": arr(f + "w2"), "b2": arr(f + "b2"), "rope": rope_tables(), "decay": decay_tables(),
    }
    nc = _bacc.Bacc("TRN2", target_bir_lowering=False, num_devices=1)
    aps = {k: nc.dram_tensor(f"in_{k}", v.shape, mybir.dt.from_np(v.dtype), kind="ExternalInput").ap()
           for k, v in arrays.items()}
    out = nc.dram_tensor("out_0", (B, L, D), F32, kind="ExternalOutput").ap()
    decoder_layer(nc, out=out, **aps)
    r = _run(nc, [{f"in_{k}": v for k, v in arrays.items()}], core_ids=[0])
    return r.results[0]["out_0"]
```

```python
from contextlib import ExitStack

import numpy as np

import concourse.bass as bass
from concourse import mybir

F32 = mybir.dt.float32
F32R = mybir.dt.float32r
ALU = mybir.AluOpType
ACT = mybir.ActivationFunctionType

P = 128
B, L, D = 16, 256, 512
NH, DH = 8, 64
HALF = DH // 2
NT = L // P
KC = D // P
E, F = 8, 2048
NM = 4
FC = F // P
SC = 4
CS = FC // SC
SLAB = F // SC
NG = 3 * NH
DW = P + L
GATE_ROW = 32
RMS_EPS, LN_EPS = 1e-6, 1e-5
DECAY, THETA = 0.9, 10000.0


class Step:

    def __init__(self, n, i=None, stride=1):
        self.n, self.i, self.stride = n, i, stride

    def __add__(self, k):
        return Step(self.n + k, self.i, self.stride)

    def __sub__(self, k):
        return self + (-k)

    def within(self, count):
        return 0 <= self.n < count

    def after(self, per, done=0):
        at = self.n * per + done
        return at if self.i is None else self.i * (self.stride * per) + at

    def pair(self, per, done=0):
        at = self.n // 2 * per + done
        return at if self.i is None else self.i * per + at

    @property
    def index(self):
        return self.after(1)

    @property
    def odd(self):
        return self.n % 2


def exact_product(eng, out, lhs_hi, lhs_lo, rhs_hi, rhs_lo, first, last):
    eng.matmul(out, lhs_hi, rhs_hi, start=first, stop=False)
    eng.matmul(out, lhs_hi, rhs_lo, start=False, stop=False)
    return eng.matmul(out, lhs_lo, rhs_hi, start=False, stop=last)


def decoder_layer(nc, x, ctx_in, norm_w, wqT, wkT, wvT, wbetaT, bbeta, wigT, big, wogT, bog,
                  woutT, bout, gamma, beta, w1, b1, w2, b2, rope, decay, out):
    x2_dram = nc.dram_tensor("x2_dram", [B * NT, P, D], F32, kind="Internal").ap()
    with ExitStack() as scope:
        attention_phase(nc, scope, x, ctx_in, norm_w, (wqT, wkT, wvT), (wbetaT, wigT, wogT),
                        (bbeta, big, bog), woutT, bout, rope, decay, x2_dram)
    with ExitStack() as scope:
        expert_phase(nc, scope, x2_dram, gamma, beta, w1, b1, w2, b2, out)


def attention_phase(nc, scope, x, ctx_in, norm_w, wT, wgT, bg, woutT, bout, rope, decay, x2_dram):
    def sb(name, shape, dt=F32):
        return scope.enter_context(nc.sbuf_tensor(name, shape, dt))

    def bank(name, cols=512):
        return scope.enter_context(nc.psum_tensor(name, [P, cols], F32))

    def sem(name):
        return scope.enter_context(nc.semaphore(name))

    wqkv_hi = sb("wqkv_hi", [P, KC, 3 * D], F32R)
    wqkv_lo = sb("wqkv_lo", [P, KC, 3 * D], F32R)
    wg_raw = sb("wg_raw", [P, KC, NG])
    wg_hi = sb("wg_hi", [P, KC, NG], F32R)
    wg_lo = sb("wg_lo", [P, KC, NG], F32R)
    wout_hi = sb("wout_hi", [P, KC, D], F32R)
    wout_lo = sb("wout_lo", [P, KC, D], F32R)
    normw = sb("normw", [P, KC])
    gate_bias = sb("gate_bias", [NG, 1])
    bout_all = sb("bout_all", [P, 1, D])
    rope_sb = sb("rope_sb", [P, NT, 2 * DH])
    decay_sb = sb("decay_sb", [P, 2, P])
    ident = sb("ident_a", [P, P])
    diag = sb("diag", [P, DW])
    head_rows_raw = sb("head_rows_raw", [DH, NH, P])
    head_rows = sb("head_rows", [DH, NH, P], F32R)
    minus_half = sb("minus_half_a", [P, NT])
    rms_eps = sb("rms_eps", [P, NT])
    ln_eps = sb("ln_eps_a", [P, NT])
    zero = sb("zero", [P, 1])
    moment = sb("moment_a", [1, 1])

    x_sb = [sb(f"x{p}", [P, NT, D]) for p in range(2)]
    c_sb = [sb(f"c{p}", [P, NT, D]) for p in range(2)]
    xb = [sb(f"xb{p}", [P, NT, D]) for p in range(2)]
    squares = sb("squares", [P, NT, D])
    sumsq = sb("sumsq", [P, NT])
    rms = sb("rms", [P, NT])
    h = sb("h", [P, NT, D])
    hT_hi = sb("hT_hi", [P, KC, L], F32R)
    hT_lo = sb("hT_lo", [P, KC, L], F32R)
    gates = sb("gates", [NG, DW])
    f_parts = sb("f_parts", [DH, DW], F32R)
    g_tok = sb("g_tok", [P, NT, NH])
    o_tok = sb("o_tok", [P, NT, NH])
    decays = sb("decays", [P, 2, NH, DW])
    rot = sb("rot", [P, 2 * NT, 2 * D])
    rot_a, rot_b = [rot[:, j, :] for j in range(NT)], [rot[:, NT + j, :] for j in range(NT)]
    v_sb = [sb(f"v{p}", [P, NT, D]) for p in range(2)]
    qkT = sb("qkT", [P, 2, KC, L])
    qT, kT = qkT[:, 0], qkT[:, 1]
    probs = sb("probs", [P, 4, DW])
    yT_hi = sb("yT_hi", [P, KC, L], F32R)
    yT_lo = sb("yT_lo", [P, KC, L], F32R)
    res = sb("res", [P, NT, D])
    stats = sb("stats_a", [P, NT, 6])
    mean_var = [sb(f"mean_var{n}", [P, NT, 2]) for n in range(2)]
    rstd = [sb(f"rstd{n}", [P, NT]) for n in range(2)]
    w_raw = [rot[:, 0:NT, :].rearrange("p j n -> p (j n)").rearrange("p (k n) -> p k n", n=D),
             rot[:, NT:2 * NT, :].rearrange("p j n -> p (j n)").rearrange("p (k n) -> p k n", n=D),
             decays[:, 1, :, :].rearrange("p h c -> p (h c)")[:, 0:KC * D].rearrange("p (k n) -> p k n", n=D)]
    wout_raw = qkT[:].rearrange("p a k t -> p (a k t)").rearrange("p (k n) -> p k n", n=D)

    turn = [bank(f"turn{n}") for n in range(2)]
    qk_ps = bank("qk_ps", 1024)
    v_ps = bank("v_ps")
    s_ps = bank("s_ps")
    y_ps = bank("y_ps")
    spread_ps = bank("spread_ps")
    out_ps = [s_ps, y_ps]

    x_in = [sem(f"x_in{p}") for p in range(2)]
    ctx_loaded = [sem(f"ctx_loaded{p}") for p in range(2)]
    w_in, tables_in, const_in = [sem(f"w_in{n}") for n in range(4)], sem("tables_in"), sem("const_in")
    ident_zero, ident_made = sem("ident_zero"), sem("ident_made")
    heads_made, w_hi, w_lo = sem("heads_made"), sem("w_hi"), sem("w_lo")
    fparts_zero = sem("fparts_zero")
    sumsq_done, rms_pre, rms_done = sem("sumsq_done"), sem("rms_pre"), sem("rms_done")
    h_done, xb_done = sem("h_done"), sem("xb_done")
    h_turned, hT_hi_done, hT_lo_done = sem("h_turned"), sem("hT_hi_done"), sem("hT_lo_done")
    gates_ps, gates_done, first_zero = sem("gates_ps"), sem("gates_done"), sem("first_zero")
    f_hi_done, f_lo_done = sem("f_hi_done"), sem("f_lo_done")
    gates_turned, gates_tok = sem("gates_turned"), sem("gates_tok")
    f_spread, decay_done = sem("f_spread"), sem("decay_done")
    v_mm, qk_mm, v_done, rope_done = sem("v_mm"), sem("qk_mm"), sem("v_done"), sem("rope_done")
    rot_done, qo_done = sem("rot_done"), sem("qo_done")
    qk_turned, qkT_done = sem("qk_turned"), sem("qkT_done")
    s_mm, probs_done = sem("s_mm"), sem("probs_done")
    y_mm, y_hi_done, y_lo_done = sem("y_mm"), sem("y_hi_done"), sem("y_lo_done")
    out_mm, res_done, stats_done = sem("out_mm"), sem("res_done"), sem("stats_done")
    mean_done = [sem(f"mean_done{n}") for n in range(2)]
    var_eps = [sem(f"var_eps{n}") for n in range(2)]
    rstd_done = [sem(f"rstd_done{n}") for n in range(2)]
    x1_done, ctx_squared, mem_mm = sem("x1_done"), sem("ctx_squared"), sem("mem_mm")
    u_done, stats2_done, x2_done, x2_stored = sem("u_done"), sem("stats2_done"), sem("x2_done"), sem("x2_stored")

    CONSTS = 7
    W_GATES = 1 + KC
    W_OF = {2: W_GATES + KC, 0: W_GATES + 2 * KC, 1: W_GATES + 3 * KC}
    W_OUT = W_GATES + 4 * KC

    def steps(eng, body):
        for n in range(-1, 2):
            body(Step(n))
        with eng.Fori(0, (B - 4) // 2) as i:
            for n in (2, 3):
                body(Step(n, i, 2))
        for n in range(B - 2, B + 2):
            body(Step(n))

    with nc.Block() as block:

        @block.sync
        def _(sp):
            def load_x(b):
                if b.n >= 2:
                    sp.wait_ge(h_done, (b - 2).after(NT, NT))
                    sp.wait_ge(xb_done, (b - 2).after(1, 1))
                sp.dma_start(x_sb[b.odd][:], x[b.index].rearrange("(j p) d -> p j d", p=P)).then_inc(x_in[b.odd], 16)

            sp.dma_start(normw[:], norm_w).then_inc(const_in, 16)
            load_x(Step(0))
            for g in range(3):
                sp.dma_start(wg_raw[:, :, g * NH:(g + 1) * NH], wgT[g].rearrange("(k p) n -> p k n", p=P)).then_inc(const_in, 16)
                sp.dma_start(gate_bias[g * NH:(g + 1) * NH, :], bg[g].rearrange("(n a) -> n a", a=1)).then_inc(const_in, 16)
            for n in (2, 0, 1):
                sp.dma_start(w_raw[n], wT[n].rearrange("(k p) n -> p k n", p=P)).then_inc(w_in[n], 16)
            sp.dma_start(rope_sb[:], rope.rearrange("(j p) c -> p j c", p=P)).then_inc(tables_in, 16)
            sp.dma_start(decay_sb[:], decay.rearrange("p (a c) -> p a c", a=2)).then_inc(tables_in, 16)
            sp.dma_start(bout_all[:, 0, :], bout.partition_broadcast(P)).then_inc(tables_in, 16)
            load_x(Step(1))
            sp.dma_start(wout_raw, woutT.rearrange("(k p) n -> p k n", p=P)).then_inc(w_in[3], 16)

            def body(b):
                if (b + 2).within(B):
                    load_x(b + 2)
                if b.within(B):
                    if b.n >= 2:
                        sp.wait_ge(mem_mm, (b - 2).after(NT, NT))
                    sp.dma_start(c_sb[b.odd][:], ctx_in[b.index].rearrange("(j p) d -> p j d", p=P)).then_inc(ctx_loaded[b.odd], 16)
                if (b - 2).within(B):
                    sp.wait_ge(x2_done, (b - 2).after(NT, NT))
                    two = (b - 2).index * NT
                    sp.dma_start(x2_dram[bass.ds(two, NT)].rearrange("j p d -> p j d"), res[:]).then_inc(x2_stored, 16)

            for n in range(0, 2):
                body(Step(n))
            with sp.Fori(0, (B - 4) // 2) as i:
                for n in (2, 3):
                    body(Step(n, i, 2))
            for n in range(B - 2, B + 2):
                body(Step(n))
            sp.wait_ge(x2_stored, 16 * B)

        @block.scalar
        def _(act):
            act.wait_ge(const_in, 16 * CONSTS)
            for k in range(KC):
                act.activation(wg_hi[:, k, :], wg_raw[:, k, :], ACT.Copy, scale=normw[:, k:k + 1]).then_inc(w_hi, 1)

            def weights_high(n):
                act.wait_ge(w_in[n], 16)
                for k in range(KC):
                    if n < 3:
                        act.activation(wqkv_hi[:, k, n * D:(n + 1) * D], w_raw[n][:, k, :], ACT.Copy,
                                       scale=normw[:, k:k + 1]).then_inc(w_hi, 1)
                    else:
                        act.activation(wout_hi[:, k, :], wout_raw[:, k, :], ACT.Copy).then_inc(w_hi, 1)

            def square_x(b):
                act.wait_ge(x_in[b.odd], b.pair(16, 16))
                if b.n >= 1:
                    act.wait_ge(rms_pre, (b - 1).after(1, 1))
                    act.wait_ge(sumsq_done, (b - 1).after(NT, NT))
                for j in range(NT):
                    act.activation(squares[:, j, :], x_sb[b.odd][:, j, :], ACT.Square,
                                   accum_out=sumsq[:, j:j + 1]).then_inc(sumsq_done, 1)

            def y_high(b):
                for c in range(KC):
                    act.wait_ge(y_mm, b.after(KC, c + 1))
                    if b.n >= 1 and c == 0:
                        act.wait_ge(out_mm, (b - 1).after(NT, NT))
                    act.activation(yT_hi[:, c, :], y_ps[:, 0:L], ACT.Copy).then_inc(y_hi_done, 1)

            def h_high(b):
                if b.n >= 1:
                    act.wait_ge(qk_mm, (b - 1).after(NT, NT))
                for j in range(NT):
                    act.wait_ge(h_turned, b.after(NT, j + 1))
                    act.activation(hT_hi[:, :, j * P:(j + 1) * P], turn[j][:].rearrange("p (k t) -> p k t", k=KC),
                                   ACT.Copy).then_inc(hT_hi_done, 1)

            def gate(b):
                act.wait_ge(gates_ps, b.after(1, 1))
                if b.n >= 1:
                    act.wait_ge(f_lo_done, (b - 1).after(1, 1))
                    act.wait_ge(gates_turned, (b - 1).after(1, 1))
                act.activation(gates[:, P:DW], v_ps[0:NG, 0:L], ACT.Sigmoid, bias=gate_bias[:]).then_inc(gates_done, 1)
                act.activation(gates[:, 0:P], v_ps[0:NG, P:L], ACT.Sigmoid, bias=gate_bias[:]).then_inc(gates_done, 1)

            def keep_qkT(b, j):
                if b.n == 0 and j == 0:
                    act.wait_ge(w_lo, W_OUT)
                if b.n >= 1 and j == 0:
                    act.wait_ge(s_mm, (b - 1).after(NH, NH))
                for n, dst in enumerate((qT, kT)):
                    act.wait_ge(qk_turned, b.after(2 * NT, 2 * j + n + 1))
                    act.activation(dst[:, :, j * P:(j + 1) * P], turn[n][:].rearrange("p (k t) -> p k t", k=KC),
                                   ACT.Copy).then_inc(qkT_done, 1)

            def body(b):
                if (b + 1).within(B):
                    square_x(b + 1)
                if (b - 1).within(B):
                    y_high(b - 1)
                if (b + 1).within(B):
                    h_high(b + 1)
                    if b.n == -1:
                        weights_high(2)
                    gate(b + 1)
                    if b.n == -1:
                        for n in (0, 1, 3):
                            weights_high(n)
                if b.within(B):
                    keep_qkT(b, 0)
                    keep_qkT(b, 1)

            steps(act, body)

        @block.gpsimd
        def _(pool):
            pool.memset(ident[:], 0.0).then_inc(ident_zero, 1)
            pool.memset(diag[:], 0.0).then_inc(ident_zero, 1)
            pool.memset(head_rows_raw[:], 0.0).then_inc(ident_zero, 1)
            pool.memset(minus_half[:], -0.5).then_inc(ident_zero, 1)
            pool.memset(zero[:], 0.0).then_inc(ident_zero, 1)
            pool.memset(rms_eps[:], D * RMS_EPS).then_inc(ident_zero, 1)
            pool.memset(ln_eps[:], LN_EPS).then_inc(ident_zero, 1)
            pool.memset(f_parts[:].bitcast(F32), 0.0).then_inc(fparts_zero, 1)
            pool.wait_ge(ident_zero, 7)
            pool.affine_select(out=ident[:], in_=ident[:], compare_op=ALU.not_equal, fill=1.0, base=0,
                               pattern=[[-1, P]], channel_multiplier=1).then_inc(ident_made, 1)
            pool.affine_select(out=diag[:, 0:P], in_=diag[:, 0:P], compare_op=ALU.not_equal, fill=1.0, base=0,
                               pattern=[[-1, P]], channel_multiplier=1).then_inc(ident_made, 1)
            pool.affine_select(out=diag[:, P:DW], in_=diag[:, P:DW], compare_op=ALU.not_equal, fill=1.0, base=0,
                               pattern=[[-1, L]], channel_multiplier=1).then_inc(ident_made, 1)
            pool.affine_select(out=head_rows_raw[:], in_=head_rows_raw[:], compare_op=ALU.not_equal, fill=1.0, base=0,
                               pattern=[[-1, NH], [0, P]], channel_multiplier=1).then_inc(heads_made, 1)
            pool.wait_ge(heads_made, 1)
            pool.affine_select(out=head_rows_raw[:], in_=head_rows_raw[:], compare_op=ALU.not_equal, fill=1.0,
                               base=-GATE_ROW, pattern=[[-1, NH], [0, P]], channel_multiplier=1).then_inc(heads_made, 1)
            pool.wait_ge(const_in, 16 * CONSTS)

            def rms_scale(b):
                pool.wait_ge(sumsq_done, b.after(NT, NT))
                if b.n >= 1:
                    pool.wait_ge(h_done, (b - 1).after(NT, NT))
                pool.tensor_tensor(rms[:], sumsq[:], rms_eps[:], ALU.add).then_inc(rms_pre, 1)
                pool.wait_ge(rms_pre, b.after(1, 1))
                pool.tensor_tensor(rms[:], rms[:], minus_half[:], ALU.pow).then_inc(rms_done, 1)

            def norm_scale(b, n):
                pool.wait_ge(mean_done[n], b.after(NT, NT))
                pool.tensor_tensor(rstd[n][:], mean_var[n][:, :, 1], ln_eps[:], ALU.add).then_inc(var_eps[n], 1)
                pool.wait_ge(var_eps[n], b.after(1, 1))
                pool.tensor_tensor(rstd[n][:], rstd[n][:], minus_half[:], ALU.pow).then_inc(rstd_done[n], 1)

            def square_ctx(b):
                pool.wait_ge(ctx_loaded[b.odd], b.pair(16, 16))
                c = c_sb[b.odd][:]
                pool.tensor_tensor(c, c, c, ALU.mult).then_inc(ctx_squared, 1)

            def rotate(b, j):
                pool.wait_ge(rope_done, b.after(NT, j + 1))
                a = rot_a[j]
                pool.tensor_tensor(a, a, rot_b[j], ALU.add).then_inc(rot_done, 1)
                pool.wait_ge(rot_done, b.after(NT, j + 1))
                q = rot_a[j][:, 0:D].rearrange("p (h d) -> p h d", h=NH)
                o = o_tok[:, j, :].unsqueeze(2).broadcast_to([P, NH, DH])
                pool.tensor_tensor(q, q, o, ALU.mult).then_inc(qo_done, 1)

            def residual(b):
                pool.wait_ge(x_in[b.odd], b.pair(16, 16))
                if b.n == 0:
                    pool.wait_ge(tables_in, 16 * 3)
                if b.n >= 2:
                    pool.wait_ge(res_done, (b - 2).after(NT, NT))
                pool.tensor_tensor(xb[b.odd][:], x_sb[b.odd][:], bout_all[:].broadcast_to([P, NT, D]), ALU.add).then_inc(xb_done, 1)

            def first_column(b):
                pool.wait_ge(gates_done, b.after(2, 2))
                first = gates[0:NH, P:P + 1]
                pool.tensor_tensor(first, first, zero[0:NH, :], ALU.mult).then_inc(first_zero, 1)

            def body(b):
                if (b + 1).within(B):
                    rms_scale(b + 1)
                if (b - 2).within(B):
                    norm_scale(b - 2, 1)
                if (b - 1).within(B):
                    square_ctx(b - 1)
                if b.within(B):
                    rotate(b, 0)
                    rotate(b, 1)
                if (b - 1).within(B):
                    norm_scale(b - 1, 0)
                if (b + 1).within(B):
                    first_column(b + 1)
                    residual(b + 1)

            steps(pool, body)

        @block.vector
        def _(dve):
            dve.wait_ge(heads_made, 2)
            dve.tensor_copy(head_rows[:], head_rows_raw[:]).then_inc(w_lo, 1)
            dve.wait_ge(const_in, 16 * CONSTS)
            for k in range(KC):
                dve.wait_ge(w_hi, k + 1)
                dve.scalar_tensor_tensor(out=wg_lo[:, k, :], in0=wg_raw[:, k, :], scalar=normw[:, k:k + 1],
                                         in1=wg_hi[:, k, :].bitcast(F32), op0=ALU.mult, op1=ALU.subtract).then_inc(w_lo, 1)

            def weights_low(n):
                for k in range(KC):
                    dve.wait_ge(w_hi, KC + (1, 2, 0, 3)[n] * KC + k + 1)
                    if n < 3:
                        cols = slice(n * D, (n + 1) * D)
                        dve.scalar_tensor_tensor(out=wqkv_lo[:, k, cols], in0=w_raw[n][:, k, :], scalar=normw[:, k:k + 1],
                                                 in1=wqkv_hi[:, k, cols].bitcast(F32), op0=ALU.mult,
                                                 op1=ALU.subtract).then_inc(w_lo, 1)
                    else:
                        dve.tensor_tensor(wout_lo[:, k, :], wout_raw[:, k, :], wout_hi[:, k, :].bitcast(F32),
                                          ALU.subtract).then_inc(w_lo, 1)

            def scale_h(b):
                dve.wait_ge(rms_done, b.after(1, 1))
                dve.wait_ge(x_in[b.odd], b.pair(16, 16))
                if b.n >= 1:
                    dve.wait_ge(h_turned, (b - 1).after(NT, NT))
                for j in range(NT):
                    dve.tensor_scalar(h[:, j, :], x_sb[b.odd][:, j, :], rms[:, j:j + 1], float(D) ** 0.5,
                                      ALU.mult, ALU.mult).then_inc(h_done, 1)

            def h_low(b):
                for j in range(NT):
                    dve.wait_ge(hT_hi_done, b.after(NT, j + 1))
                    cols = slice(j * P, (j + 1) * P)
                    dve.tensor_tensor(hT_lo[:, :, cols], turn[j][:].rearrange("p (k t) -> p k t", k=KC),
                                      hT_hi[:, :, cols].bitcast(F32), ALU.subtract).then_inc(hT_lo_done, 1)

            def split_gates(b):
                dve.wait_ge(first_zero, b.after(1, 1))
                if b.n >= 1:
                    dve.wait_ge(f_spread, (b - 1).after(NH, NH))
                else:
                    dve.wait_ge(fparts_zero, 1)
                dve.tensor_copy(f_parts[0:NH, :], gates[0:NH, :]).then_inc(f_hi_done, 1)
                dve.wait_ge(f_hi_done, b.after(1, 1))
                dve.tensor_tensor(f_parts[GATE_ROW:GATE_ROW + NH, :], gates[0:NH, :], f_parts[0:NH, :].bitcast(F32),
                                  ALU.subtract).then_inc(f_lo_done, 1)

            def token_gates(b):
                dve.wait_ge(gates_turned, b.after(1, 1))
                if b.n >= 1:
                    dve.wait_ge(v_done, (b - 1).after(NT, NT))
                    dve.wait_ge(qo_done, (b - 1).after(NT, NT))
                tok = v_ps[:, L:L + NT * NG].rearrange("p (j g) -> p j g", g=NG)
                dve.tensor_scalar(g_tok[:], tok[:, :, NH:2 * NH], float(DH) ** -0.5, None, ALU.mult).then_inc(gates_tok, 1)
                dve.tensor_copy(o_tok[:], tok[:, :, 2 * NH:NG]).then_inc(gates_tok, 1)

            def scan(b, n):
                dve.wait_ge(f_spread, b.after(NH, n + 1))
                if b.n >= 2 and n == 0:
                    dve.wait_ge(probs_done, (b - 2).after(NH, NH))
                dve.tensor_tensor_scan(decays[:, b.odd, n, :], spread_ps[:, 0:DW], diag[:], 0.0, ALU.mult, ALU.add).then_inc(decay_done, 1)

            def gate_v(b, j):
                dve.wait_ge(v_mm, b.after(NT, j + 1))
                dve.wait_ge(gates_tok, b.after(2, 2))
                if b.n >= 2 and j == 0:
                    dve.wait_ge(y_mm, (b - 2).after(KC, KC))
                dve.tensor_tensor(v_sb[b.odd][:, j, :].rearrange("p (h d) -> p h d", h=NH),
                                  v_ps[:].rearrange("p (h d) -> p h d", h=NH),
                                  g_tok[:, j, :].unsqueeze(2).broadcast_to([P, NH, DH]), ALU.mult).then_inc(v_done, 1)

            def rope_parts(b, j):
                dve.wait_ge(qk_mm, b.after(NT, j + 1))
                if b.n >= 1:
                    dve.wait_ge(qk_turned, (b - 1).after(2 * NT, 2 * NT))
                src = qk_ps[:].rearrange("p (h d) -> p h d", d=DH)
                a = rot_a[j].rearrange("p (h d) -> p h d", d=DH)
                s = rot_b[j].rearrange("p (h d) -> p h d", d=DH)

                def table(lo, hi):
                    return rope_sb[:, j:j + 1, lo:hi].broadcast_to([P, 2 * NH, hi - lo])

                dve.tensor_tensor(a, src, table(0, DH), ALU.mult)
                dve.tensor_tensor(s[:, :, 0:HALF], src[:, :, HALF:DH], table(DH, DH + HALF), ALU.mult)
                dve.tensor_tensor(s[:, :, HALF:DH], src[:, :, 0:HALF], table(DH + HALF, 2 * DH), ALU.mult).then_inc(rope_done, 1)

            def weigh(b, n):
                dve.wait_ge(s_mm, b.after(NH, n + 1))
                dve.wait_ge(decay_done, b.after(NH, n + 1))
                if n >= 4:
                    dve.wait_ge(y_mm, b.after(KC, (n - 4) // 2 + 1))
                elif b.n >= 1:
                    dve.wait_ge(y_mm, (b - 1).after(KC, (n + 4) // 2 + 1))
                dve.tensor_tensor(probs[:, n % 4, :], s_ps[:, 0:DW], decays[:, b.odd, n, :], ALU.mult).then_inc(probs_done, 1)

            def y_low(b, c):
                dve.wait_ge(y_hi_done, b.after(KC, c + 1))
                dve.tensor_tensor(yT_lo[:, c, :], y_ps[:, 0:L], yT_hi[:, c, :].bitcast(F32),
                                  ALU.subtract).then_inc(y_lo_done, 1)

            def add_residual(b):
                if b.n >= 1:
                    dve.wait_ge(x2_stored, (b - 1).after(16, 16))
                dve.wait_ge(xb_done, b.after(1, 1))
                for j in range(NT):
                    dve.wait_ge(out_mm, b.after(NT, j + 1))
                    dve.tensor_tensor(res[:, j, :], out_ps[j][:], xb[b.odd][:, j, :], ALU.add).then_inc(res_done, 1)

            def norm_stats(b, n):
                made, seen = ((res_done, stats_done), (u_done, stats2_done))[n]
                for j in range(NT):
                    dve.wait_ge(made, b.after(NT, j + 1))
                    dve.bn_stats(stats[:, j, :], res[:, j, :]).then_inc(seen, 1)
                dve.wait_ge(seen, b.after(NT, NT))
                dve.memset(moment[:], 0.0)
                for j in range(NT):
                    dve.bn_aggr(mean_var[n][:, j, :], stats[:, j, :]).then_inc(mean_done[n], 1)

            def normalize(b, n):
                dve.wait_ge(rstd_done[n], b.after(1, 1))
                for j in range(NT):
                    dve.tensor_scalar(res[:, j, :], res[:, j, :], mean_var[n][:, j, 0:1], rstd[n][:, j:j + 1],
                                      ALU.subtract, ALU.mult).then_inc((x1_done, x2_done)[n], 1)

            def add_memory(b):
                for j in range(NT):
                    dve.wait_ge(mem_mm, b.after(NT, j + 1))
                    dve.wait_ge(x1_done, b.after(NT, j + 1))
                    dve.scalar_tensor_tensor(out=res[:, j, :], in0=qk_ps[:, j * D:(j + 1) * D], scalar=1.0,
                                             in1=res[:, j, :], op0=ALU.add, op1=ALU.mult).then_inc(u_done, 1)

            def body(b):
                if (b - 2).within(B):
                    add_memory(b - 2)
                    norm_stats(b - 2, 1)
                for n in range(NH):
                    if b.within(B) and n == 1:
                        gate_v(b, 0)
                    if b.within(B) and n == 5:
                        gate_v(b, 1)
                    if (b - 1).within(B) and n in (2, 4, 6):
                        y_low(b - 1, n // 2 - 1)
                    if (b - 1).within(B):
                        weigh(b - 1, n)
                    if (b - 2).within(B) and n == 1:
                        normalize(b - 2, 1)
                    if b.within(B):
                        scan(b, n)
                    if (b + 1).within(B) and n == 6:
                        scale_h(b + 1)
                    if b.within(B) and n == 3:
                        rope_parts(b, 0)
                    if b.within(B) and n == 7:
                        rope_parts(b, 1)
                if (b - 1).within(B):
                    y_low(b - 1, KC - 1)
                if (b + 1).within(B):
                    h_low(b + 1)
                if b.n == -1:
                    weights_low(2)
                if (b - 1).within(B):
                    add_residual(b - 1)
                    norm_stats(b - 1, 0)
                if (b + 1).within(B):
                    split_gates(b + 1)
                if (b - 1).within(B):
                    normalize(b - 1, 0)
                if (b + 1).within(B):
                    token_gates(b + 1)
                if b.n == -1:
                    for n in (0, 1, 3):
                        weights_low(n)
                    dve.wait_ge(w_lo, W_OUT)
                    dve.wait_ge(tables_in, 16 * 3)

            steps(dve, body)

        @block.tensor
        def _(pe):
            def turn_h(b):
                if b.n >= 2:
                    pe.wait_ge(qkT_done, (b - 2).after(2 * NT, 2 * NT))
                else:
                    pe.wait_ge(ident_made, 3)
                for j in range(NT):
                    pe.wait_ge(h_done, b.after(NT, j + 1))
                    for k in range(KC):
                        mm = pe.transpose(turn[j][:, k * P:(k + 1) * P], h[:, j, k * P:(k + 1) * P], ident[:])
                    mm.then_inc(h_turned, 1)

            def gate_products(b):
                if b.n == 0:
                    pe.wait_ge(w_lo, W_GATES)
                else:
                    pe.wait_ge(v_done, (b - 1).after(NT, NT))
                pe.wait_ge(hT_lo_done, b.after(NT, NT))
                for k in range(KC):
                    mm = exact_product(pe, v_ps[0:NG, 0:L], wg_hi[:, k, :], wg_lo[:, k, :],
                                       hT_hi[:, k, :], hT_lo[:, k, :], k == 0, k == KC - 1)
                mm.then_inc(gates_ps, 1)

            def turn_gates(b):
                pe.wait_ge(first_zero, b.after(1, 1))
                for j in range(NT):
                    mm = pe.matmul(v_ps[:, L + j * NG:L + (j + 1) * NG], gates[:, (j + 1) * P:(j + 2) * P],
                                   ident[0:NG, 0:NG], start=True, stop=True)
                mm.then_inc(gates_turned, 1)

            def spread_f(b, n):
                if n == 0:
                    pe.wait_ge(f_lo_done, b.after(1, 1))
                if n >= 1 or b.n >= 1:
                    pe.wait_ge(decay_done, b.after(NH, n))
                pe.matmul(spread_ps[:, 0:DW], head_rows[:, n, :], f_parts[:], start=True, stop=True).then_inc(f_spread, 1)

            def project_share(b, g):
                j, n, k = g // (3 * KC), (2, 0, 1)[g // KC % 3], g % KC
                dst = v_ps[:] if n == 2 else qk_ps[:, n * D:(n + 1) * D]
                if k == 0 and n == 2 and j == 0:
                    pe.wait_ge(gates_tok, b.after(2, 2))
                elif k == 0 and n == 2:
                    pe.wait_ge(v_done, b.after(NT, 1))
                elif k == 0 and n == 0 and j == 0 and b.n >= 2:
                    pe.wait_ge(u_done, (b - 2).after(NT, NT))
                elif k == 0 and n == 0 and j == 1:
                    pe.wait_ge(rope_done, b.after(NT, 1))
                if b.n == 0 and k == 0 and j == 0:
                    pe.wait_ge(w_lo, W_OF[n])
                tok = slice(j * P, (j + 1) * P)
                mm = exact_product(pe, dst, hT_hi[:, k, tok], hT_lo[:, k, tok],
                                   wqkv_hi[:, k, n * D:(n + 1) * D], wqkv_lo[:, k, n * D:(n + 1) * D],
                                   k == 0, k == KC - 1)
                if k == KC - 1 and n == 2:
                    mm.then_inc(v_mm, 1)
                if k == KC - 1 and n == 1:
                    mm.then_inc(qk_mm, 1)

            def turn_qk(b, j):
                    pe.wait_ge(qo_done, b.after(NT, j + 1))
                    for n in range(2):
                        if j == 1:
                            pe.wait_ge(qkT_done, b.after(2 * NT, n + 1))
                        elif (b + 1).within(B):
                            pe.wait_ge(hT_lo_done, (b + 1).after(NT, NT))
                        for k in range(KC):
                            mm = pe.transpose(turn[n][:, k * P:(k + 1) * P],
                                              rot_a[j][:, n * D + k * P:n * D + (k + 1) * P], ident[:])
                        mm.then_inc(qk_turned, 1)

            def scores(b, n):
                rows, c = slice(n % 2 * DH, (n % 2 + 1) * DH), n // 2
                if n == 0:
                    pe.wait_ge(qkT_done, b.after(2 * NT, 2 * NT))
                if n >= 1:
                    pe.wait_ge(probs_done, b.after(NH, n))
                elif b.n >= 1:
                    pe.wait_ge(res_done, (b - 1).after(NT, 1))
                pe.matmul(s_ps[:, 0:P], kT[rows, c, P:L], qT[rows, c, P:L], start=True, stop=True)
                pe.matmul(s_ps[:, P:DW], kT[rows, c, 0:P], qT[rows, c, 0:L], start=True, stop=True).then_inc(s_mm, 1)

            def weighted_values(b, c):
                if c >= 1:
                    pe.wait_ge(y_lo_done, b.after(KC, c))
                elif b.n >= 1:
                    pe.wait_ge(res_done, (b - 1).after(NT, NT))
                v = v_sb[b.odd]
                pe.wait_ge(probs_done, b.after(NH, 2 * c + 2))
                for n in (2 * c, 2 * c + 1):
                    rows = slice(n % 2 * DH, (n % 2 + 1) * DH)
                    pe.matmul(y_ps[rows, 0:L], v[:, 0, n * DH:(n + 1) * DH], probs[:, n % 4, P:DW],
                              start=True, stop=False)
                for n in (2 * c, 2 * c + 1):
                    rows = slice(n % 2 * DH, (n % 2 + 1) * DH)
                    mm = pe.matmul(y_ps[rows, P:L], v[:, 1, n * DH:(n + 1) * DH], probs[:, n % 4, 0:P],
                                   start=False, stop=True)
                mm.then_inc(y_mm, 1)

            def slot(b, n):
                if b.within(B):
                    project_share(b, 3 * n)
                    project_share(b, 3 * n + 1)
                if (b - 1).within(B):
                    scores(b - 1, n)
                if b.within(B):
                    project_share(b, 3 * n + 2)
                    spread_f(b, n)
                if (b - 1).within(B) and n % 2 == 1:
                    weighted_values(b - 1, n // 2)

            def project_out(b):
                if b.n == 0:
                    pe.wait_ge(w_lo, W_OUT)
                for j in range(NT):
                    if j == 0:
                        pe.wait_ge(probs_done, b.after(NH, NH))
                    for k in range(KC):
                        if j == 0:
                            pe.wait_ge(y_lo_done, b.after(KC, k + 1))
                        tok = slice(j * P, (j + 1) * P)
                        mm = exact_product(pe, out_ps[j][:], yT_hi[:, k, tok], yT_lo[:, k, tok],
                                           wout_hi[:, k, :], wout_lo[:, k, :], k == 0, k == KC - 1)
                    mm.then_inc(out_mm, 1)

            def cross_memory(b):
                if b.n == 0:
                    pe.wait_ge(tables_in, 16 * 3)
                pe.wait_ge(ctx_squared, b.after(1, 1))
                if (b + 1).within(B):
                    pe.wait_ge(rope_done, (b + 1).after(NT, NT))
                c = c_sb[b.odd]
                pe.matmul(qk_ps[:, 0:D], decay_sb[:, 0, :], c[:, 0, :], start=True, stop=True).then_inc(mem_mm, 1)
                pe.matmul(qk_ps[:, D:2 * D], decay_sb[:, 1, :], c[:, 0, :], start=True, stop=False)
                pe.matmul(qk_ps[:, D:2 * D], decay_sb[:, 0, :], c[:, 1, :], start=False, stop=True).then_inc(mem_mm, 1)

            def body(b):
                for n in range(NH):
                    slot(b, n)
                if (b + 1).within(B):
                    turn_h(b + 1)
                if (b - 1).within(B):
                    project_out(b - 1)
                if (b + 1).within(B):
                    gate_products(b + 1)
                if b.within(B):
                    turn_qk(b, 0)
                if (b - 1).within(B):
                    cross_memory(b - 1)
                if (b + 1).within(B):
                    turn_gates(b + 1)
                if b.within(B):
                    turn_qk(b, 1)

            steps(pe, body)


def expert_phase(nc, scope, x2_dram, gamma, beta, w1, b1, w2, b2, out):
    def sb(name, shape, dt=F32):
        return scope.enter_context(nc.sbuf_tensor(name, shape, dt))

    def bank(name):
        return scope.enter_context(nc.psum_tensor(name, [P, 512], F32))

    def sem(name):
        return scope.enter_context(nc.semaphore(name))

    x2_view = x2_dram.rearrange("(m t) p d -> t p m d", t=E)
    out_view = out.rearrange("b (j p) d -> (b j) p d", p=P).rearrange("(m t) p d -> t p m d", t=E)
    T = NM * P

    ident = sb("ident_b", [P, P])
    minus_half = sb("minus_half_b", [P, NM])
    ln_eps = sb("ln_eps_b", [P, NM])
    moment = sb("moment_b", [1, 1])
    gamma_sb = sb("gamma_sb", [P, KC])
    beta_sb = sb("beta_sb", [P, KC])
    b1_cols = sb("b1_cols", [P, E * FC])
    w1_raw = [sb(f"w1_raw{s}", [P, KC, SLAB]) for s in range(2)]
    w2_raw = [sb(f"w2_raw{s}", [P, CS, D]) for s in range(2)]
    w1_hi = [sb(f"w1_hi{s}", [P, KC, SLAB], F32R) for s in range(2)]
    w1_lo = [sb(f"w1_lo{s}", [P, KC, SLAB], F32R) for s in range(2)]
    w2_hi = [sb(f"w2_hi{s}", [P, CS, D], F32R) for s in range(2)]
    w2_lo = [sb(f"w2_lo{s}", [P, CS, D], F32R) for s in range(2)]
    x2 = sb("x2", [P, NM, D])
    x2b = sb("x2b", [P, NM, D])
    b2_all = sb("b2_all", [P, 1, D])
    xn = sb("xn", [P, NM, D])
    xnT = sb("xnT", [P, KC, T])
    xnT_hi = sb("xnT_hi", [P, KC, T], F32R)
    xnT_lo = sb("xnT_lo", [P, KC, T], F32R)
    hid = [sb(f"hid{n}", [P, T]) for n in range(2)]
    hid_hi = [sb(f"hid_hi{n}", [P, T], F32R) for n in range(2)]
    hid_lo = [sb(f"hid_lo{n}", [P, T], F32R) for n in range(2)]
    res = sb("res_b", [P, NM, D])
    stats = [sb(f"stats_b{n}", [P, NM, 6]) for n in range(2)]
    mean_var = [sb(f"mean_var_b{n}", [P, NM, 2]) for n in range(2)]
    rstd = [sb(f"rstd_b{n}", [P, NM]) for n in range(2)]

    acc = [bank(f"acc{m}") for m in range(NM)]
    up_ps = [bank(f"up{n}") for n in range(2)]
    turn = [bank(f"turn_b{n}") for n in range(2)]

    const_in, ident_made, ident_zero = sem("const_in_b"), sem("ident_made_b"), sem("ident_zero_b")
    w1_in = [sem(f"w1_in{s}") for s in range(2)]
    w2_in = [sem(f"w2_in{s}") for s in range(2)]
    w1_hi_done, w1_lo_done = sem("w1_hi_done"), sem("w1_lo_done")
    w2_hi_done, w2_lo_done = sem("w2_hi_done"), sem("w2_lo_done")
    x2_in, b2_in, x2b_done = sem("x2_in"), sem("b2_in"), sem("x2b_done")
    x2b_half = sem("x2b_half")
    stats_done = [sem(f"stats_done_b{n}") for n in range(2)]
    mean_done = [sem(f"mean_done_b{n}") for n in range(2)]
    var_eps = [sem(f"var_eps_b{n}") for n in range(2)]
    rstd_done = [sem(f"rstd_done_b{n}") for n in range(2)]
    xn_done, xn_turned, xnT_done = sem("xn_done"), sem("xn_turned"), sem("xnT_done")
    xnT_hi_done, xnT_lo_done = sem("xnT_hi_done"), sem("xnT_lo_done")
    up_mm, down_mm, gelu_done = sem("up_mm"), sem("down_mm"), sem("gelu_done")
    tile_mm = sem("tile_mm")
    hid_hi_done, hid_lo_done = sem("hid_hi_done"), sem("hid_lo_done")
    res_done, out_done, out_stored = sem("res_done_b"), sem("out_done"), sem("out_stored")

    def experts(eng, body):
        with eng.Fori(0, E - 1) as i:
            body(Step(0, i), True)
        body(Step(E - 1), False)

    def slab(e, s):
        return (e + s // SC), s % SC

    with nc.Block() as block:

        @block.sync
        def _(sp):
            def load_slab(e, s):
                e, s = slab(e, s)
                if not (e.i is None and e.n == 0 and s < 2):
                    sp.wait_ge(w1_lo_done, e.after(SC, s - 1))
                    sp.wait_ge(w2_lo_done, e.after(SC, s - 1))
                    sp.wait_ge(w1_hi_done, e.after(SC, s - 1))
                    sp.wait_ge(w2_hi_done, e.after(SC, s - 1))
                sp.dma_start(w1_raw[s % 2][:], w1[e.index].rearrange("(k p) f -> p k f", p=P)[:, :, s * SLAB:(s + 1) * SLAB])\
                    .then_inc(w1_in[s % 2], 16)
                sp.dma_start(w2_raw[s % 2][:], w2[e.index].rearrange("(s c p) d -> s p c d", p=P, c=CS)[s])\
                    .then_inc(w2_in[s % 2], 16)

            def load_tokens(e):
                sp.dma_start(x2[:], x2_view[e.index]).then_inc(x2_in, 16)
                sp.dma_start(b2_all[:, 0, :], b2[e.index].partition_broadcast(P)).then_inc(b2_in, 16)

            load_tokens(Step(0))
            sp.dma_start(gamma_sb[:], gamma).then_inc(const_in, 16)
            sp.dma_start(beta_sb[:], beta).then_inc(const_in, 16)
            sp.dma_start(b1_cols[:], b1).then_inc(const_in, 16)
            load_slab(Step(0), 0)
            load_slab(Step(0), 1)

            def store(e):
                sp.wait_ge(out_done, e.after(NM, NM))
                sp.dma_start(out_view[e.index], res[:]).then_inc(out_stored, 16)

            def body(e, more):
                load_slab(e, 2)
                if more:
                    sp.wait_ge(x2b_done, e.after(1, 1))
                    load_tokens(e + 1)
                load_slab(e, 3)
                if more:
                    load_slab(e, 4)
                    load_slab(e, 5)
                    store(e)

            experts(sp, body)
            last = Step(E - 1)
            for m in range(NM):
                sp.wait_ge(out_done, last.after(NM, m + 1))
                sp.dma_start(out_view[last.index, :, m, :], res[:, m, :]).then_inc(out_stored, 16)
            sp.wait_ge(out_stored, 16 * (E - 1 + NM))

        @block.scalar
        def _(act):
            def split_w1(e, s):
                e, s = slab(e, s)
                act.wait_ge(w1_in[s % 2], e.after(16 * SC // 2, 16 * (s // 2 + 1)))
                if not (e.i is None and e.n == 0 and s < 2):
                    act.wait_ge(up_mm, e.after(FC, CS * (s - 1)))
                act.activation(w1_hi[s % 2][:], w1_raw[s % 2][:], ACT.Copy).then_inc(w1_hi_done, 1)

            def split_w2(e, s):
                e, s = slab(e, s)
                act.wait_ge(w2_in[s % 2], e.after(16 * SC // 2, 16 * (s // 2 + 1)))
                if not (e.i is None and e.n == 0 and s < 2):
                    act.wait_ge(down_mm, e.after(FC, CS * (s - 1)))
                act.activation(w2_hi[s % 2][:], w2_raw[s % 2][:], ACT.Copy).then_inc(w2_hi_done, 1)

            def split_tokens(e):
                for k in range(KC):
                    act.wait_ge(xnT_done, e.after(KC, k + 1))
                    if k == 0 and not (e.i is None and e.n == 0):
                        act.wait_ge(up_mm, e.after(FC, 0))
                    act.activation(xnT_hi[:, k, :], xnT[:, k, :], ACT.Copy).then_inc(xnT_hi_done, 1)

            def gelu(e, c):
                act.wait_ge(up_mm, e.after(FC, c + 1))
                if c >= 2 or not (e.i is None and e.n == 0):
                    act.wait_ge(hid_lo_done, e.after(FC, c - 1))
                act.activation(hid[c % 2][:], up_ps[c % 2][:], ACT.Gelu,
                               bias=b1_cols[:, bass.ds(e.after(FC, c), 1)]).then_inc(gelu_done, 1)

            split_w1(Step(0), 0)
            split_w2(Step(0), 0)
            act.wait_ge(const_in, 16 * 3)
            split_tokens(Step(0))

            def body(e, more):
                for c in range(FC):
                    if c == FC - 1 and more:
                        split_tokens(e + 1)
                    gelu(e, c)
                    if c % CS == 0 and (more or c // CS + 1 < SC):
                        split_w1(e, c // CS + 1)
                    if c % CS == 1 and (more or c // CS + 1 < SC):
                        split_w2(e, c // CS + 1)

            def peeled(e, more):
                body(e, more)

            body(Step(0), True)
            with act.Fori(0, E - 2) as i:
                body(Step(1, i), True)
            peeled(Step(E - 1), False)

        @block.gpsimd
        def _(pool):
            pool.memset(ident[:], 0.0).then_inc(ident_zero, 1)
            pool.memset(minus_half[:], -0.5).then_inc(ident_zero, 1)
            pool.memset(ln_eps[:], LN_EPS).then_inc(ident_zero, 1)
            pool.wait_ge(ident_zero, 3)
            pool.affine_select(out=ident[:], in_=ident[:], compare_op=ALU.not_equal, fill=1.0, base=0,
                               pattern=[[-1, P]], channel_multiplier=1).then_inc(ident_made, 1)

            def norm_scale(e, n):
                pool.wait_ge(mean_done[n], e.after(NM, NM))
                pool.tensor_tensor(rstd[n][:], mean_var[n][:, :, 1], ln_eps[:], ALU.add).then_inc(var_eps[n], 1)
                pool.wait_ge(var_eps[n], e.after(1, 1))
                pool.tensor_tensor(rstd[n][:], rstd[n][:], minus_half[:], ALU.pow).then_inc(rstd_done[n], 1)

            def add_b2(e):
                pool.wait_ge(x2_in, e.after(16, 16))
                pool.wait_ge(b2_in, e.after(16, 16))
                pool.wait_ge(xn_done, e.after(NM, NM))
                if e.n >= 1:
                    pool.wait_ge(res_done, e.after(NM, 0))
                pool.tensor_tensor(x2b[:], x2[:], b2_all[:].broadcast_to([P, NM, D]), ALU.add).then_inc(x2b_half, 1)
                pool.wait_ge(x2b_half, e.after(1, 1))
                pool.tensor_tensor(x2b[:], x2b[:], x2[:], ALU.add).then_inc(x2b_done, 1)

            def split_w2(e, s):
                e, s = slab(e, s)
                pool.wait_ge(w2_hi_done, e.after(SC, s + 1))
                pool.tensor_tensor(w2_lo[s % 2][:], w2_raw[s % 2][:], w2_hi[s % 2][:].bitcast(F32), ALU.subtract)\
                    .then_inc(w2_lo_done, 1)

            norm_scale(Step(0), 0)
            split_w2(Step(0), 0)

            def body(e, more):
                if e.n >= 1:
                    norm_scale(e - 1, 1)
                add_b2(e)
                for s in range(SC):
                    if more or s + 1 < SC:
                        split_w2(e, s + 1)
                    if s == 1 and more:
                        norm_scale(e + 1, 0)

            body(Step(0), True)
            with pool.Fori(0, E - 2) as i:
                body(Step(1, i), True)
            body(Step(E - 1), False)
            last = Step(E - 1)
            for m in range(NM):
                pool.wait_ge(mean_done[1], last.after(NM, m + 1))
                scale = rstd[1][:, m:m + 1]
                pool.tensor_tensor(scale, mean_var[1][:, m, 1:2], ln_eps[:, m:m + 1], ALU.add).then_inc(var_eps[1], 1)
                pool.wait_ge(var_eps[1], last.after(1, m + 1))
                pool.tensor_tensor(scale, scale, minus_half[:, m:m + 1], ALU.pow).then_inc(rstd_done[1], 1)

        @block.vector
        def _(dve):
            def norm_stats(e, n):
                src = (x2, res)[n]
                if n == 0:
                    dve.wait_ge(x2_in, e.after(16, 16))
                for m in range(NM):
                    if n == 1:
                        dve.wait_ge(res_done, e.after(NM, m + 1))
                    dve.bn_stats(stats[n][:, m, :], src[:, m, :]).then_inc(stats_done[n], 1)
                dve.wait_ge(stats_done[n], e.after(NM, NM))
                dve.memset(moment[:], 0.0)
                for m in range(NM):
                    dve.bn_aggr(mean_var[n][:, m, :], stats[n][:, m, :]).then_inc(mean_done[n], 1)

            def normalize(e, n):
                src, dst = ((x2, xn), (res, res))[n]
                dve.wait_ge(rstd_done[n], e.after(1, 1))
                if n == 0 and e.n >= 1:
                    dve.wait_ge(xn_turned, e.after(KC, 0))
                for m in range(NM):
                    dve.tensor_scalar(dst[:, m, :], src[:, m, :], mean_var[n][:, m, 0:1], rstd[n][:, m:m + 1],
                                      ALU.subtract, ALU.mult).then_inc((xn_done, out_done)[n], 1)

            def affine(e, k):
                dve.wait_ge(xn_turned, e.after(KC, k + 1))
                if e.n >= 1 and k == 0:
                    dve.wait_ge(xnT_hi_done, e.after(KC, 0))
                    dve.wait_ge(xnT_lo_done, e.after(KC, 0))
                dve.tensor_scalar(xnT[:, k, :], turn[k % 2][:], gamma_sb[:, k:k + 1], beta_sb[:, k:k + 1],
                                  ALU.mult, ALU.add).then_inc(xnT_done, 1)

            def tokens_low(e):
                for k in range(KC):
                    dve.wait_ge(xnT_hi_done, e.after(KC, k + 1))
                    dve.tensor_tensor(xnT_lo[:, k, :], xnT[:, k, :], xnT_hi[:, k, :].bitcast(F32), ALU.subtract)\
                        .then_inc(xnT_lo_done, 1)

            def split_w1(e, s):
                e, s = slab(e, s)
                dve.wait_ge(w1_hi_done, e.after(SC, s + 1))
                dve.tensor_tensor(w1_lo[s % 2][:], w1_raw[s % 2][:], w1_hi[s % 2][:].bitcast(F32), ALU.subtract)\
                    .then_inc(w1_lo_done, 1)

            def split_hidden(e, c):
                dve.wait_ge(gelu_done, e.after(FC, c + 1))
                if c >= 2 or e.n >= 1:
                    dve.wait_ge(down_mm, e.after(FC, c - 1))
                dve.tensor_copy(hid_hi[c % 2][:], hid[c % 2][:]).then_inc(hid_hi_done, 1)
                dve.wait_ge(hid_hi_done, e.after(FC, c + 1))
                dve.tensor_tensor(hid_lo[c % 2][:], hid[c % 2][:], hid_hi[c % 2][:].bitcast(F32), ALU.subtract)\
                    .then_inc(hid_lo_done, 1)

            def finish(e):
                dve.wait_ge(out_stored, e.after(16, 0))
                for m in range(NM):
                    dve.wait_ge(tile_mm, m + 1)
                    dve.tensor_tensor(res[:, m, :], acc[m][:], x2b[:, m, :], ALU.add).then_inc(res_done, 1)
                    dve.wait_ge(res_done, e.after(NM, m + 1))
                    dve.bn_stats(stats[1][:, m, :], res[:, m, :]).then_inc(stats_done[1], 1)
                    dve.wait_ge(stats_done[1], e.after(NM, m + 1))
                    dve.bn_aggr(mean_var[1][:, m, :], stats[1][:, m, :]).then_inc(mean_done[1], 1)
                    if m >= 1:
                        finish_norm(e, m - 1)
                finish_norm(e, NM - 1)

            def finish_norm(e, m):
                dve.wait_ge(rstd_done[1], e.after(1, m + 1))
                dve.tensor_scalar(res[:, m, :], res[:, m, :], mean_var[1][:, m, 0:1], rstd[1][:, m:m + 1],
                                  ALU.subtract, ALU.mult).then_inc(out_done, 1)

            def add_residual(e):
                dve.wait_ge(down_mm, e.after(FC, FC))
                dve.wait_ge(x2b_done, e.after(1, 1))
                if e.n >= 1:
                    dve.wait_ge(out_stored, e.after(16, 0))
                for m in range(NM):
                    dve.tensor_tensor(res[:, m, :], acc[m][:], x2b[:, m, :], ALU.add).then_inc(res_done, 1)

            norm_stats(Step(0), 0)
            split_w1(Step(0), 0)
            normalize(Step(0), 0)
            dve.wait_ge(const_in, 16 * 3)
            for k in range(KC):
                affine(Step(0), k)
            tokens_low(Step(0))

            def body(e, more):
                for c in range(FC):
                    if c == FC - 1 and more:
                        tokens_low(e + 1)
                    split_hidden(e, c)
                    if e.n >= 1:
                        if c == 0:
                            add_residual(e - 1)
                        if c == 1:
                            norm_stats(e - 1, 1)
                        if c == 3:
                            normalize(e - 1, 1)
                    if c % CS == 2 and (more or c // CS + 1 < SC):
                        split_w1(e, c // CS + 1)
                    if more:
                        if c == 8:
                            norm_stats(e + 1, 0)
                        if c == 9:
                            normalize(e + 1, 0)
                        if 11 <= c < 11 + KC:
                            affine(e + 1, c - 11)

            body(Step(0), True)
            body(Step(1), True)
            with dve.Fori(0, E - 3) as i:
                body(Step(2, i), True)
            body(Step(E - 1), False)
            finish(Step(E - 1))

        @block.tensor
        def _(pe):
            def turn_tokens(e, k):
                if k == 0:
                    pe.wait_ge(xn_done, e.after(NM, NM))
                if k >= 2 or e.n >= 1:
                    pe.wait_ge(xnT_done, e.after(KC, k - 1))
                for m in range(NM):
                    mm = pe.transpose(turn[k % 2][:, m * P:(m + 1) * P], xn[:, m, k * P:(k + 1) * P], ident[:])
                mm.then_inc(xn_turned, 1)

            def up(e, c):
                s = c // CS
                if c % CS == 0:
                    pe.wait_ge(w1_lo_done, e.after(SC, s + 1))
                if c >= 2 or e.n >= 1:
                    pe.wait_ge(gelu_done, e.after(FC, c - 1))
                cols = slice(c % CS * P, (c % CS + 1) * P)
                for k in range(KC):
                    if c == 0:
                        pe.wait_ge(xnT_lo_done, e.after(KC, k + 1))
                    mm = exact_product(pe, up_ps[c % 2][:], w1_hi[s % 2][:, k, cols], w1_lo[s % 2][:, k, cols],
                                       xnT_hi[:, k, :], xnT_lo[:, k, :], k == 0, k == KC - 1)
                mm.then_inc(up_mm, 1)

            def down(e, c, tiles=False):
                s = c // CS
                if c % CS == 0:
                    pe.wait_ge(w2_lo_done, e.after(SC, s + 1))
                pe.wait_ge(hid_lo_done, e.after(FC, c + 1))
                for m in range(NM):
                    if c == 0 and (e.n >= 1):
                        pe.wait_ge(res_done, e.after(NM, m + 1 - NM))
                    tok = slice(m * P, (m + 1) * P)
                    mm = exact_product(pe, acc[m][:], hid_hi[c % 2][:, tok], hid_lo[c % 2][:, tok],
                                       w2_hi[s % 2][:, c % CS, :], w2_lo[s % 2][:, c % CS, :], c == 0, c == FC - 1)
                    if tiles:
                        mm.then_inc(tile_mm, 1)
                if not tiles:
                    mm.then_inc(down_mm, 1)

            pe.wait_ge(ident_made, 1)
            for k in range(KC):
                turn_tokens(Step(0), k)
            up(Step(0), 0)

            def body(e, more):
                for c in range(1, FC):
                    up(e, c)
                    down(e, c - 1)
                    if more and 11 <= c < 11 + KC:
                        turn_tokens(e + 1, c - 11)
                if more:
                    up(e + 1, 0)
                down(e, FC - 1, tiles=not more)

            body(Step(0), True)
            with pe.Fori(0, E - 2) as i:
                body(Step(1, i), True)
            body(Step(E - 1), False)


def rope_tables():
    half = np.arange(HALF, dtype=np.float32) / np.float32(HALF)
    inv_freq = np.float32(1.0) / np.float32(THETA) ** half
    angles = np.arange(L, dtype=np.float32)[:, None] * inv_freq[None, :]
    cos, sin = np.cos(angles), np.sin(angles)
    return np.ascontiguousarray(np.concatenate([cos, cos, -sin, sin], axis=1), np.float32)


def decay_tables():
    step = np.arange(P)[None, :] - np.arange(P)[:, None]
    base = float(np.float32(DECAY))
    within = np.where(step >= 0, base ** np.maximum(step, 0), 0.0)
    return np.ascontiguousarray(np.concatenate([within, base ** (step + P)], axis=1), np.float32)


def kernel(**inputs):
    import concourse.bacc as _bacc
    from concourse.bass_utils import run_bass_kernel_spmd as _run

    def arr(name):
        return np.ascontiguousarray(inputs[name])

    def turned(name):
        return np.ascontiguousarray(np.asarray(inputs[name]).T)

    def columns(name):
        return np.ascontiguousarray(np.asarray(inputs[name]).reshape(-1, P).T)

    a = "L0_attn_"
    f = "L0_ffn_"
    arrays = {
        "x": arr("x"), "ctx_in": arr("ctx_1024"), "norm_w": columns(a + "norm_w"),
        "wqT": turned(a + "Wq"), "wkT": turned(a + "Wk"), "wvT": turned(a + "Wv"),
        "wbetaT": turned(a + "Wbeta"), "bbeta": arr(a + "bbeta"), "wigT": turned(a + "Wig"), "big": arr(a + "big"),
        "wogT": turned(a + "Wog"), "bog": arr(a + "bog"), "woutT": turned(a + "Wout"), "bout": arr(a + "bout"),
        "gamma": columns(f + "gamma"), "beta": columns(f + "beta"), "w1": arr(f + "w1"), "b1": columns(f + "b1"),
        "w2": arr(f + "w2"), "b2": arr(f + "b2"), "rope": rope_tables(), "decay": decay_tables(),
    }
    nc = _bacc.Bacc("TRN2", target_bir_lowering=False, num_devices=1)
    aps = {k: nc.dram_tensor(f"in_{k}", v.shape, mybir.dt.from_np(v.dtype), kind="ExternalInput").ap()
           for k, v in arrays.items()}
    out = nc.dram_tensor("out_0", (B, L, D), F32, kind="ExternalOutput").ap()
    decoder_layer(nc, out=out, **aps)
    r = _run(nc, [{f"in_{k}": v for k, v in arrays.items()}], core_ids=[0])
    return r.results[0]["out_0"]
```

```python
from contextlib import ExitStack

import numpy as np

import concourse.bass as bass
from concourse import mybir

F32 = mybir.dt.float32
F32R = mybir.dt.float32r
ALU = mybir.AluOpType
ACT = mybir.ActivationFunctionType

P = 128
B, L, D = 16, 256, 512
NH, DH = 8, 64
HALF = DH // 2
NT = L // P
KC = D // P
WARM_UP = 13
E, F = 8, 2048
NM = 4
FC = F // P
SC = 4
CS = FC // SC
SLAB = F // SC
NG = 3 * NH
SCANS = {3: (0,), 4: (1, 2), 5: (3, 4, 5), 6: (6, 7)}
LOW_ROW = 32
DW = P + L
RMS_EPS, LN_EPS = 1e-6, 1e-5
DECAY, THETA = 0.9, 10000.0


class Step:

    def __init__(self, n, i=None, stride=1):
        self.n, self.i, self.stride = n, i, stride

    def __add__(self, k):
        return Step(self.n + k, self.i, self.stride)

    def __sub__(self, k):
        return self + (-k)

    def within(self, count):
        return 0 <= self.n < count

    def after(self, per, done=0):
        at = self.n * per + done
        return at if self.i is None else self.i * (self.stride * per) + at

    def pair(self, per, done=0):
        at = self.n // 2 * per + done
        return at if self.i is None else self.i * per + at

    @property
    def index(self):
        return self.after(1)

    @property
    def odd(self):
        return self.n % 2


def exact_product(eng, out, lhs_hi, lhs_lo, rhs_hi, rhs_lo, first, last):
    eng.matmul(out, lhs_hi, rhs_hi, start=first, stop=False)
    eng.matmul(out, lhs_hi, rhs_lo, start=False, stop=False)
    return eng.matmul(out, lhs_lo, rhs_hi, start=False, stop=last)


def decoder_layer(nc, x, ctx_in, norm_w, wqT, wkT, wvT, wbetaT, bbeta, wigT, big, wogT, bog,
                  woutT, bout, gamma, beta, w1, b1, w2, b2, rope, decay, out):
    with ExitStack() as scope:
        layer_program(nc, scope, x, ctx_in, norm_w, (wqT, wkT, wvT), (wbetaT, wigT, wogT), (bbeta, big, bog),
                      woutT, bout, gamma, beta, w1, b1, w2, b2, rope, decay, out)


def layer_program(nc, scope, x, ctx_in, norm_w, wT, wgT, bg, woutT, bout, gamma, beta, w1, b1, w2, b2,
                  rope, decay, out):
    f_dram = nc.dram_tensor("f_dram", [2, NH * L], F32, kind="Internal").ap()
    x2_dram = nc.dram_tensor("x2_dram", [B * NT, P, D], F32, kind="Internal").ap()
    x2_view = x2_dram.rearrange("(m t) p d -> t p m d", t=E)
    out_view = out.rearrange("b (j p) d -> (b j) p d", p=P).rearrange("(m t) p d -> t p m d", t=E)
    T = NM * P

    def sb(name, shape, dt=F32):
        return scope.enter_context(nc.sbuf_tensor(name, shape, dt))

    def bank(name, cols=512):
        return scope.enter_context(nc.psum_tensor(name, [P, cols], F32))

    def sem(name):
        return scope.enter_context(nc.semaphore(name))

    wqkv_hi = sb("wqkv_hi", [P, KC, 3 * D], F32R)
    wqkv_lo = sb("wqkv_lo", [P, KC, 3 * D], F32R)
    wg_raw = sb("wg_raw", [P, KC, NG])
    wg_parts = sb("wg_parts", [P, KC, LOW_ROW + NG], F32R)
    wg_hi, wg_lo = wg_parts[:, :, 0:NG], wg_parts[:, :, LOW_ROW:]
    wout_hi = sb("wout_hi", [P, KC, D], F32R)
    wout_lo = sb("wout_lo", [P, KC, D], F32R)
    normw = sb("normw", [P, KC])
    gate_bias = sb("gate_bias", [NG, 1])
    bout_all = sb("bout_all", [P, 1, D])
    rope_sb = sb("rope_sb", [P, NT, 2 * DH])
    memory_raw = sb("memory_raw", [P, 2 * P + 2 * NT])
    shrink, grow = memory_raw[:, 2 * P:2 * P + NT], memory_raw[:, 2 * P + NT:]
    sums = sb("sums", [P, 2, P], F32R)
    ident = sb("ident", [P, P])
    diag = sb("diag", [P, DW])
    minus_half = sb("minus_half_a", [P, NT])
    rms_eps = sb("rms_eps", [P, NT])
    ln_eps = sb("ln_eps_a", [P, NT])
    one = sb("one", [P, 1])
    warm = sb("warm", [P, 1])
    moment = sb("moment", [1, 1])

    x_both = sb("x_both", [P, 2 * NT, D])
    c_both = sb("c_both", [P, 2 * NT, D])
    xb_both = sb("xb_both", [P, 2 * NT, D])
    x_sb = [x_both[:, p * NT:(p + 1) * NT, :] for p in range(2)]
    c_sb = [c_both[:, p * NT:(p + 1) * NT, :] for p in range(2)]
    xb = [xb_both[:, p * NT:(p + 1) * NT, :] for p in range(2)]
    h_squares = sb("h_squares", [P, 2 * NT, D])
    h, squares = h_squares[:, 0:NT, :], h_squares[:, NT:2 * NT, :]
    sumsq = sb("sumsq", [P, NT])
    rms = sb("rms", [P, NT])
    hT = sb("hT", [P, 2, KC, L], F32R)
    hT_hi, hT_lo = hT[:, 0], hT[:, 1]
    gates = sb("gates", [NG, L])
    gates_low = sb("gates_low", [NG, L])
    gates_sum = sb("gates_sum", [NG, L])
    f_all = sb("f_all", [P, NH, L])
    g_tok = sb("g_tok", [P, NT, NH])
    o_tok = sb("o_tok", [P, 2, NT, NH])
    decays = sb("decays", [P, 2, NH, DW])
    rot = sb("rot", [P, 2 * NT, 2 * D])
    rot_a, rot_b = [rot[:, j, :] for j in range(NT)], [rot[:, NT + j, :] for j in range(NT)]
    v_sb = [sb(f"v{p}", [P, NT, D]) for p in range(2)]
    qkT = sb("qkT", [P, 2, KC, L])
    qT, kT = qkT[:, 0], qkT[:, 1]
    probs = sb("probs", [P, 4, DW])
    yT_hi = sb("yT_hi", [P, KC, L], F32R)
    yT_lo = sb("yT_lo", [P, KC, L], F32R)
    ctx_parts = sb("ctx_parts", [P, 2 * NT, D], F32R)
    ctx_hi, ctx_lo = ctx_parts[:, 0:NT, :], ctx_parts[:, NT:2 * NT, :]
    res = sb("res", [P, NT, D])
    stats = sb("stats_a", [P, NT, 6])
    mean_var = [sb(f"mean_var{n}", [P, NT, 2]) for n in range(2)]
    rstd = [sb(f"rstd{n}", [P, NT]) for n in range(2)]
    w_raw = [rot[:, 0:NT, :].rearrange("p j n -> p (j n)").rearrange("p (k n) -> p k n", n=D),
             rot[:, NT:2 * NT, :].rearrange("p j n -> p (j n)").rearrange("p (k n) -> p k n", n=D),
             decays[:, 1, :, :].rearrange("p h c -> p (h c)")[:, 0:KC * D].rearrange("p (k n) -> p k n", n=D)]
    wout_raw = qkT[:].rearrange("p a k t -> p (a k t)").rearrange("p (k n) -> p k n", n=D)

    turn = [bank(f"turn{n}") for n in range(2)]
    qk_ps = bank("qk_ps", 1024)
    v_ps = bank("v_ps")
    s_ps = bank("s_ps")
    y_ps = bank("y_ps")
    gate_ps = bank("gate_ps")
    out_ps = [s_ps, y_ps]

    x_in = [sem(f"x_in{p}") for p in range(2)]
    ctx_loaded = [sem(f"ctx_loaded{p}") for p in range(2)]
    w_in, tables_in, const_in = [sem(f"w_in{n}") for n in range(4)], sem("tables_in"), sem("const_in")
    ident_zero, ident_made, sums_made = sem("ident_zero"), sem("ident_made"), sem("sums_made")
    w_hi, w_lo = sem("w_hi"), sem("w_lo")
    sumsq_done, rms_pre, rms_done = sem("sumsq_done"), sem("rms_pre"), sem("rms_done")
    h_done, xb_done = sem("h_done"), sem("xb_done")
    h_turned, hT_hi_done, hT_lo_done = sem("h_turned"), sem("hT_hi_done"), sem("hT_lo_done")
    gates_ps, gates_done = sem("gates_ps"), sem("gates_done")
    gates_low_out, gates_summed, wg_zero = sem("gates_low_out"), sem("gates_summed"), sem("wg_zero")
    gates_turned, gates_tok = sem("gates_turned"), sem("gates_tok")
    f_stored, f_in, decay_done = sem("f_stored"), sem("f_in"), sem("decay_done")
    v_mm, qk_mm, v_done, rope_done = sem("v_mm"), sem("qk_mm"), sem("v_done"), sem("rope_done")
    rot_done, qo_done = sem("rot_done"), sem("qo_done")
    qk_turned, qkT_done = sem("qk_turned"), sem("qkT_done")
    s_mm, probs_done = sem("s_mm"), sem("probs_done")
    y_mm, y_hi_done, y_lo_done = sem("y_mm"), sem("y_hi_done"), sem("y_lo_done")
    out_mm, res_done, stats_done = sem("out_mm"), sem("res_done"), sem("stats_done")
    mean_done = [sem(f"mean_done{n}") for n in range(2)]
    var_eps = [sem(f"var_eps{n}") for n in range(2)]
    rstd_done = [sem(f"rstd_done{n}") for n in range(2)]
    x1_done, ctx_squared, mem_mm = sem("x1_done"), sem("ctx_squared"), sem("mem_mm")
    ctx_hi_done, ctx_lo_done, mem_grown = sem("ctx_hi_done"), sem("ctx_lo_done"), sem("mem_grown")
    u_done, stats2_done, x2_done, x2_stored = sem("u_done"), sem("stats2_done"), sem("x2_done"), sem("x2_stored")

    CONSTS = 7
    W_GATES = KC
    W_OF = {2: W_GATES + KC, 0: W_GATES + 2 * KC, 1: W_GATES + 3 * KC}
    W_OUT = W_GATES + 4 * KC

    def score_banks(b):
        return (s_ps, gate_ps) if b.n == B - 1 and b.i is None else turn

    def memory(b):
        return (turn[0][:], turn[1][:]) if b.n == B - 1 and b.i is None else (qk_ps[:, 0:D], qk_ps[:, D:2 * D])

    def steps(eng, body):
        for n in range(-1, 2):
            body(Step(n))
        with eng.Fori(0, (B - 4) // 2) as i:
            for n in (2, 3):
                body(Step(n, i, 2))
        for n in range(B - 2, B + 2):
            body(Step(n))

    e_minus_half = sb("minus_half_b", [P, NM])
    e_ln_eps = sb("ln_eps_b", [P, NM])
    gamma_sb = sb("gamma_sb", [P, KC])
    beta_sb = sb("beta_sb", [P, KC])
    b1_cols = sb("b1_cols", [P, E * FC])

    def on(tensor, letters, lo, inner):
        flat = tensor.rearrange(f"p {letters} -> p ({letters})")
        return flat[:, lo:lo + 4 * inner].rearrange("p (k n) -> p k n", n=inner)

    x2 = x_both[:]
    xn, xnT = on(rot[:], "j n", 0, D), on(rot[:], "j n", NM * D, T)
    xnT_hi, xnT_lo = [on(w[:], "k n", 0, T) for w in (wqkv_hi, wqkv_lo)]
    x2b = c_both[:]
    e_res = xb_both[:]
    b2_all = v_sb[0][:, 0:1, :]
    hid = [v_sb[0][:, 1, :], bout_all[:, 0, :]]
    hid_hi, hid_lo = [[on_y.rearrange("p k t -> p (k t)")[:, n * T:(n + 1) * T] for n in range(2)]
                      for on_y in (yT_hi[:], yT_lo[:])]
    w1_raw = [h_squares[:], on(decays[:, 1], "h c", 0, SLAB)]
    w2_raw = [on(decays[:, 0], "h c", 0, D), on(qkT[:], "a k t", 0, D)]
    w1_hi = [on(wqkv_hi[:], "k n", KC * T, SLAB), on(hT[:], "a k t", 0, SLAB)]
    w1_lo = [on(wqkv_lo[:], "k n", KC * T, SLAB), ctx_parts[:]]
    w2_hi = [on(wqkv_hi[:], "k n", KC * (T + SLAB), D), wout_hi[:]]
    w2_lo = [on(wqkv_lo[:], "k n", KC * (T + SLAB), D), wout_lo[:]]
    e_stats = [sb(f"stats_b{n}", [P, NM, 6]) for n in range(2)]
    e_mean_var = [sb(f"mean_var_b{n}", [P, NM, 2]) for n in range(2)]
    e_rstd = [sb(f"rstd_b{n}", [P, NM]) for n in range(2)]

    acc = [s_ps, y_ps, qk_ps[:, 0:D], qk_ps[:, D:2 * D]]
    up_ps = [v_ps, gate_ps]

    e_const_in = sem("const_in_b")
    w1_in = [sem(f"w1_in{s}") for s in range(2)]
    w2_in = [sem(f"w2_in{s}") for s in range(2)]
    w1_hi_done, w1_lo_done = sem("w1_hi_done"), sem("w1_lo_done")
    w2_hi_done, w2_lo_done = sem("w2_hi_done"), sem("w2_lo_done")
    x2_in, b2_in, x2b_done = sem("x2_in"), sem("b2_in"), sem("x2b_done")
    x2b_half = sem("x2b_half")
    e_stats_done = [sem(f"stats_done_b{n}") for n in range(2)]
    e_mean_done = [sem(f"mean_done_b{n}") for n in range(2)]
    e_var_eps = [sem(f"var_eps_b{n}") for n in range(2)]
    e_rstd_done = [sem(f"rstd_done_b{n}") for n in range(2)]
    xn_done, xn_turned, xnT_done = sem("xn_done"), sem("xn_turned"), sem("xnT_done")
    xnT_hi_done, xnT_lo_done = sem("xnT_hi_done"), sem("xnT_lo_done")
    up_mm, down_mm, gelu_done = sem("up_mm"), sem("down_mm"), sem("gelu_done")
    tile_mm = sem("tile_mm")
    hid_hi_done, hid_lo_done = sem("hid_hi_done"), sem("hid_lo_done")
    e_res_done, out_done, out_stored = sem("res_done_b"), sem("out_done"), sem("out_stored")

    def late(e, c):
        return e.i is None and e.n == E - 1 and c >= FC - CS

    def hidden_parts(e, c):
        if late(e, c):
            return w1_hi[0][:, c % CS, :], w1_lo[0][:, c % CS, :]
        return hid_hi[c % 2][:], hid_lo[c % 2][:]

    def slab(e, s):
        return (e + s // SC), s % SC

    with nc.Block() as block:

        @block.sync
        def _(sp):
            def load_x(b):
                if b.n >= 2:
                    sp.wait_ge(h_done, (b - 2).after(NT, NT))
                    sp.wait_ge(xb_done, (b - 2).after(1, 1))
                sp.dma_start(x_sb[b.odd][:], x[b.index].rearrange("(j p) d -> p j d", p=P)).then_inc(x_in[b.odd], 16)

            sp.dma_start(normw[:], norm_w).then_inc(const_in, 16)
            load_x(Step(0))
            for g in range(3):
                sp.dma_start(wg_raw[:, :, g * NH:(g + 1) * NH], wgT[g].rearrange("(k p) n -> p k n", p=P)).then_inc(const_in, 16)
                sp.dma_start(gate_bias[g * NH:(g + 1) * NH, :], bg[g].rearrange("(n a) -> n a", a=1)).then_inc(const_in, 16)
            for n in (2, 0, 1):
                sp.dma_start(w_raw[n], wT[n].rearrange("(k p) n -> p k n", p=P)).then_inc(w_in[n], 16)
            sp.dma_start(rope_sb[:], rope.rearrange("(j p) c -> p j c", p=P)).then_inc(tables_in, 16)
            sp.dma_start(memory_raw[:], decay).then_inc(tables_in, 16)
            sp.dma_start(bout_all[:, 0, :], bout.partition_broadcast(P)).then_inc(tables_in, 16)
            load_x(Step(1))

            def spread_f(b):
                sp.wait_ge(gates_done, b.after(1, 1))
                sp.dma_start(f_dram[b.odd].rearrange("(h t) -> h t", h=NH), gates[0:NH, :]).then_inc(f_stored, 16)
                sp.wait_ge(f_stored, b.after(16, 16))
                sp.dma_start(f_all[:].rearrange("p h t -> p (h t)"), f_dram[b.odd].partition_broadcast(P)).then_inc(f_in, 16)

            spread_f(Step(0))
            sp.dma_start(wout_raw, woutT.rearrange("(k p) n -> p k n", p=P)).then_inc(w_in[3], 16)
            sp.dma_start(gamma_sb[:], gamma).then_inc(e_const_in, 16)
            sp.dma_start(beta_sb[:], beta).then_inc(e_const_in, 16)
            sp.dma_start(b1_cols[:], b1).then_inc(e_const_in, 16)

            def body(b):
                if (b + 2).within(B):
                    load_x(b + 2)
                if b.within(B):
                    if b.n >= 2:
                        sp.wait_ge(u_done, (b - 2).after(NT, NT))
                    sp.dma_start(c_sb[b.odd][:], ctx_in[b.index].rearrange("(j p) d -> p j d", p=P)).then_inc(ctx_loaded[b.odd], 16)
                if (b - 2).within(B):
                    sp.wait_ge(x2_done, (b - 2).after(NT, NT))
                    two = (b - 2).index * NT
                    sp.dma_start(x2_dram[bass.ds(two, NT)].rearrange("j p d -> p j d"), res[:]).then_inc(x2_stored, 16)
                if (b + 1).within(B):
                    spread_f(b + 1)

            def load_slab(e, s):
                e, s = slab(e, s)
                sp.wait_ge(w1_lo_done, e.after(SC, s - 1))
                sp.wait_ge(w2_lo_done, e.after(SC, s - 1))
                sp.wait_ge(w1_hi_done, e.after(SC, s - 1))
                sp.wait_ge(w2_hi_done, e.after(SC, s - 1))
                load_w1(e, s)
                load_w2(e, s)

            def load_w1(e, s):
                sp.dma_start(w1_raw[s % 2][:], w1[e.index].rearrange("(k p) f -> p k f", p=P)[:, :, s * SLAB:(s + 1) * SLAB])\
                    .then_inc(w1_in[s % 2], 16)

            def load_w2(e, s):
                sp.dma_start(w2_raw[s % 2][:], w2[e.index].rearrange("(s c p) d -> s p c d", p=P, c=CS)[s])\
                    .then_inc(w2_in[s % 2], 16)

            def load_tokens(e):
                sp.dma_start(x2[:], x2_view[e.index]).then_inc(x2_in, 16)

            def load_b2(e):
                sp.dma_start(b2_all[:, 0, :], b2[e.index].partition_broadcast(P)).then_inc(b2_in, 16)

            def store(e):
                sp.wait_ge(out_done, e.after(NM, NM))
                sp.dma_start(out_view[e.index], e_res[:]).then_inc(out_stored, 16)

            def expert(e, more):
                load_slab(e, 2)
                if more:
                    sp.wait_ge(x2b_done, e.after(1, 1))
                    load_tokens(e + 1)
                    load_b2(e + 1)
                load_slab(e, 3)
                if more:
                    load_slab(e, 4)
                    load_slab(e, 5)
                    store(e)

            for n in range(0, 2):
                body(Step(n))
            with sp.Fori(0, (B - 4) // 2) as i:
                for n in (2, 3):
                    body(Step(n, i, 2))
            body(Step(B - 2))
            body(Step(B - 1))
            ahead, last = Step(0), Step(B - 1)
            sp.wait_ge(h_done, last.after(NT, NT))
            sp.wait_ge(xb_done, last.after(1, 1))
            sp.wait_ge(x2_stored, 16 * (B - 3))
            load_tokens(ahead)
            sp.wait_ge(h_turned, last.after(NT, NT))
            sp.wait_ge(sumsq_done, last.after(NT, NT))
            load_w1(ahead, 0)
            sp.wait_ge(probs_done, (last - 1).after(NH, NH))
            load_w2(ahead, 0)
            sp.wait_ge(y_mm, (last - 1).after(KC, KC))
            load_b2(ahead)
            body(Step(B))
            sp.wait_ge(probs_done, last.after(NH, NH))
            load_w1(ahead, 1)
            sp.wait_ge(s_mm, last.after(NH, NH))
            load_w2(ahead, 1)
            body(Step(B + 1))
            sp.wait_ge(x2_stored, 16 * B)

            with sp.Fori(0, E - 1) as i:
                expert(Step(0, i), True)
            expert(Step(E - 1), False)
            last = Step(E - 1)
            for m in range(NM):
                sp.wait_ge(out_done, last.after(NM, m + 1))
                sp.dma_start(out_view[last.index, :, m, :], e_res[:, m, :]).then_inc(out_stored, 16)
            sp.wait_ge(out_stored, 16 * (E - 1 + NM))

        @block.scalar
        def _(act):
            def square_x(b):
                act.wait_ge(x_in[b.odd], b.pair(16, 16))
                if b.n >= 1:
                    act.wait_ge(rms_pre, (b - 1).after(1, 1))
                    act.wait_ge(sumsq_done, (b - 1).after(NT, NT))
                for j in range(NT):
                    act.activation(squares[:, j, :], x_sb[b.odd][:, j, :], ACT.Square,
                                   accum_out=sumsq[:, j:j + 1]).then_inc(sumsq_done, 1)

            act.wait_ge(ident_zero, 8)
            act.activation(warm[:], one[:], ACT.Sigmoid)
            square_x(Step(0))
            act.wait_ge(const_in, 16 * CONSTS)
            for k in range(KC):
                act.activation(wg_hi[:, k, :], wg_raw[:, k, :], ACT.Copy, scale=normw[:, k:k + 1]).then_inc(w_hi, 1)

            def weights_high(n):
                act.wait_ge(w_in[n], 16)
                for k in range(KC):
                    if n < 3:
                        act.activation(wqkv_hi[:, k, n * D:(n + 1) * D], w_raw[n][:, k, :], ACT.Copy,
                                       scale=normw[:, k:k + 1]).then_inc(w_hi, 1)
                    else:
                        act.activation(wout_hi[:, k, :], wout_raw[:, k, :], ACT.Copy).then_inc(w_hi, 1)

            def y_high(b, c):
                act.wait_ge(y_mm, b.after(KC, c + 1))
                if b.n >= 1 and c == 0:
                    act.wait_ge(out_mm, (b - 1).after(NT, NT))
                act.activation(yT_hi[:, c, :], y_ps[:, 0:L], ACT.Copy).then_inc(y_hi_done, 1)

            def h_high(b):
                if b.n >= 1:
                    act.wait_ge(qk_mm, (b - 1).after(NT, NT))
                for j in range(NT):
                    act.wait_ge(h_turned, b.after(NT, j + 1))
                    act.activation(hT_hi[:, :, j * P:(j + 1) * P], turn[j][:].rearrange("p (k t) -> p k t", k=KC),
                                   ACT.Copy).then_inc(hT_hi_done, 1)

            def gate_low(b):
                act.wait_ge(gates_ps, b.after(1, 1))
                if b.n >= 1:
                    act.wait_ge(gates_summed, (b - 1).after(1, 1))
                act.activation(gates_low[:], gate_ps[LOW_ROW:LOW_ROW + NG, 0:L], ACT.Copy).then_inc(gates_low_out, 1)

            def gate(b):
                act.wait_ge(gates_summed, b.after(1, 1))
                if b.n >= 1:
                    act.wait_ge(f_stored, (b - 1).after(16, 16))
                    act.wait_ge(decay_done, (b - 1).after(NH, NH))
                    act.wait_ge(gates_turned, (b - 1).after(1, 1))
                act.activation(gates[:], gates_sum[:], ACT.Sigmoid, bias=gate_bias[:]).then_inc(gates_done, 1)

            def keep_qkT(b, j):
                if b.n == 0 and j == 0:
                    act.wait_ge(w_lo, W_OUT)
                if b.n >= 1 and j == 0:
                    act.wait_ge(s_mm, (b - 1).after(NH, NH))
                for n, dst in enumerate((qT, kT)):
                    act.wait_ge(qk_turned, b.after(2 * NT, 2 * j + n + 1))
                    act.activation(dst[:, :, j * P:(j + 1) * P], turn[n][:].rearrange("p (k t) -> p k t", k=KC),
                                   ACT.Copy).then_inc(qkT_done, 1)

            def square_ctx(b):
                act.wait_ge(ctx_loaded[b.odd], b.pair(16, 16))
                if b.n == 0:
                    act.wait_ge(tables_in, 16 * 3)
                for j in range(NT):
                    c = c_sb[b.odd][:, j, :]
                    act.activation(c, c, ACT.Square, scale=shrink[:, j:j + 1]).then_inc(ctx_squared, 1)
                act.wait_ge(ctx_squared, b.after(NT, NT))
                act.activation(ctx_hi, c_sb[b.odd][:], ACT.Copy).then_inc(ctx_hi_done, 1)

            def grow_memory(b):
                for j in range(NT):
                    act.wait_ge(mem_mm, b.after(NT, j + 1))
                    if j == 0:
                        act.wait_ge(ctx_lo_done, b.after(1, 1))
                    act.activation(c_sb[b.odd][:, j, :], memory(b)[j], ACT.Identity, bias=one[:],
                                   scale=grow[:, j:j + 1]).then_inc(mem_grown, 1)

            def body(b):
                if (b + 1).within(B) and b.n >= 0:
                    square_x(b + 1)
                if b.n == 0:
                    weights_high(3)
                if b.n == B:
                    act.wait_ge(e_const_in, 16 * 3)
                    first_affine(0)
                    first_affine(1)
                for c in range(KC):
                    if (b - 1).within(B):
                        y_high(b - 1, c)
                    if b.n == B and c < 2:
                        token_high(Step(0), 2 * c)
                        token_high(Step(0), 2 * c + 1)
                    if b.n == B and c == 0:
                        first_affine(2)
                        first_affine(3)
                    if b.n == B and c == 2:
                        split_w2(Step(0), 0)
                if (b + 1).within(B):
                    h_high(b + 1)
                    if b.n == -1:
                        weights_high(2)
                    gate_low(b + 1)
                    if b.n == -1:
                        gate(b + 1)
                    if b.n == -1:
                        for n in (0, 1):
                            weights_high(n)
                if b.n == B - 1:
                    split_w1(Step(0), 0)
                if b.within(B):
                    keep_qkT(b, 0)
                if b.within(B) and (b + 1).within(B):
                    gate(b + 1)
                if b.within(B):
                    keep_qkT(b, 1)
                if (b - 1).within(B):
                    grow_memory(b - 1)
                if b.within(B):
                    square_ctx(b)

            def split_w1(e, s):
                e, s = slab(e, s)
                act.wait_ge(w1_in[s % 2], e.after(16 * SC // 2, 16 * (s // 2 + 1)))
                if e.i is None and e.n == 0 and s < 2:
                    act.wait_ge(qk_mm, NT * B)
                else:
                    act.wait_ge(up_mm, e.after(FC, CS * (s - 1)))
                act.activation(w1_hi[s % 2][:], w1_raw[s % 2][:], ACT.Copy).then_inc(w1_hi_done, 1)

            def split_w2(e, s):
                e, s = slab(e, s)
                act.wait_ge(w2_in[s % 2], e.after(16 * SC // 2, 16 * (s // 2 + 1)))
                if e.i is None and e.n == 0 and s < 2:
                    if s == 1:
                        act.wait_ge(out_mm, NT * B)
                else:
                    act.wait_ge(down_mm, e.after(FC, CS * (s - 1)))
                act.activation(w2_hi[s % 2][:], w2_raw[s % 2][:], ACT.Copy).then_inc(w2_hi_done, 1)

            def first_affine(k):
                act.wait_ge(xn_turned, k + 1)
                act.activation(xnT[:, k, :], turn[k % 2][:], ACT.Identity, bias=beta_sb[:, k:k + 1],
                               scale=gamma_sb[:, k:k + 1]).then_inc(xnT_done, 1)

            def token_high(e, k):
                act.wait_ge(xnT_done, e.after(KC, k + 1))
                if k == 0 and not (e.i is None and e.n == 0):
                    act.wait_ge(up_mm, e.after(FC, 0))
                act.activation(xnT_hi[:, k, :], xnT[:, k, :], ACT.Copy).then_inc(xnT_hi_done, 1)

            def gelu(e, c):
                act.wait_ge(up_mm, e.after(FC, c + 1))
                if c >= 2 or not (e.i is None and e.n == 0):
                    act.wait_ge(hid_lo_done, e.after(FC, c - 1))
                act.activation(hid[c % 2][:], up_ps[c % 2][:], ACT.Gelu,
                               bias=b1_cols[:, bass.ds(e.after(FC, c), 1)]).then_inc(gelu_done, 1)

            def expert(e, more):
                for c in range(FC):
                    if c == FC - 1 and more:
                        for k in range(KC):
                            token_high(e + 1, k)
                    gelu(e, c)
                    if c % CS == 0 and (more or c // CS + 1 < SC):
                        split_w1(e, c // CS + 1)
                    if c % CS == 1 and (more or c // CS + 1 < SC):
                        split_w2(e, c // CS + 1)

            steps(act, body)
            expert(Step(0), True)
            with act.Fori(0, E - 2) as i:
                expert(Step(1, i), True)
            expert(Step(E - 1), False)

        @block.gpsimd
        def _(pool):
            pool.memset(ident[:], 0.0).then_inc(ident_zero, 1)
            pool.memset(diag[:], 0.0).then_inc(ident_zero, 1)
            pool.memset(minus_half[:], -0.5).then_inc(ident_zero, 1)
            pool.memset(one[:], 1.0).then_inc(ident_zero, 1)
            pool.memset(rms_eps[:], D * RMS_EPS).then_inc(ident_zero, 1)
            pool.memset(ln_eps[:], LN_EPS).then_inc(ident_zero, 1)
            pool.memset(e_minus_half[:], -0.5).then_inc(ident_zero, 1)
            pool.memset(e_ln_eps[:], LN_EPS).then_inc(ident_zero, 1)
            pool.memset(wg_parts[:, :, NG:LOW_ROW].bitcast(F32), 0.0).then_inc(wg_zero, 1)
            pool.wait_ge(ident_zero, 8)
            pool.affine_select(out=ident[:], in_=ident[:], compare_op=ALU.not_equal, fill=1.0, base=0,
                               pattern=[[-1, P]], channel_multiplier=1).then_inc(ident_made, 1)
            pool.affine_select(out=diag[:, 0:P], in_=diag[:, 0:P], compare_op=ALU.not_equal, fill=1.0, base=0,
                               pattern=[[-1, P]], channel_multiplier=1).then_inc(ident_made, 1)
            pool.affine_select(out=diag[:, P:DW], in_=diag[:, P:DW], compare_op=ALU.not_equal, fill=1.0, base=0,
                               pattern=[[-1, L]], channel_multiplier=1).then_inc(ident_made, 1)
            pool.wait_ge(const_in, 16 * CONSTS)

            def rms_scale(b):
                pool.wait_ge(sumsq_done, b.after(NT, NT))
                if b.n >= 1:
                    pool.wait_ge(h_done, (b - 1).after(NT, NT))
                pool.tensor_tensor(rms[:], sumsq[:], rms_eps[:], ALU.add).then_inc(rms_pre, 1)
                pool.wait_ge(rms_pre, b.after(1, 1))
                pool.tensor_tensor(rms[:], rms[:], minus_half[:], ALU.pow).then_inc(rms_done, 1)

            def norm_scale(b, n):
                pool.wait_ge(mean_done[n], b.after(NT, NT))
                pool.tensor_tensor(rstd[n][:], mean_var[n][:, :, 1], ln_eps[:], ALU.add).then_inc(var_eps[n], 1)
                pool.wait_ge(var_eps[n], b.after(1, 1))
                pool.tensor_tensor(rstd[n][:], rstd[n][:], minus_half[:], ALU.pow).then_inc(rstd_done[n], 1)

            def context_low(b):
                pool.wait_ge(ctx_hi_done, b.after(1, 1))
                if b.n >= 1:
                    pool.wait_ge(mem_mm, (b - 1).after(NT, NT))
                pool.tensor_tensor(ctx_lo, c_sb[b.odd][:], ctx_hi.bitcast(F32), ALU.subtract).then_inc(ctx_lo_done, 1)

            def rotate(b, j):
                pool.wait_ge(rope_done, b.after(NT, j + 1))
                a = rot_a[j]
                pool.tensor_tensor(a, a, rot_b[j], ALU.add).then_inc(rot_done, 1)
                pool.wait_ge(rot_done, b.after(NT, j + 1))
                q = rot_a[j][:, 0:D].rearrange("p (h d) -> p h d", h=NH)
                o = o_tok[:, b.odd, j, :].unsqueeze(2).broadcast_to([P, NH, DH])
                pool.tensor_tensor(q, q, o, ALU.mult).then_inc(qo_done, 1)

            def residual(b):
                pool.wait_ge(x_in[b.odd], b.pair(16, 16))
                if b.n == 0:
                    pool.wait_ge(tables_in, 16 * 3)
                if b.n >= 2:
                    pool.wait_ge(res_done, (b - 2).after(NT, NT))
                pool.tensor_tensor(xb[b.odd][:], x_sb[b.odd][:], bout_all[:].broadcast_to([P, NT, D]), ALU.add).then_inc(xb_done, 1)

            def body(b):
                if (b + 1).within(B):
                    rms_scale(b + 1)
                if (b - 2).within(B):
                    norm_scale(b - 2, 1)
                if (b - 1).within(B):
                    context_low(b - 1)
                if b.n == B:
                    split_w2(Step(0), 0)
                if b.within(B):
                    rotate(b, 0)
                    rotate(b, 1)
                if b.n == B - 1:
                    expert_scale(Step(0), 0)
                if (b - 1).within(B):
                    norm_scale(b - 1, 0)
                if b.n == B - 1:
                    first_w1_low()
                if (b + 1).within(B):
                    residual(b + 1)

            def expert_scale(e, n):
                pool.wait_ge(e_mean_done[n], e.after(NM, NM))
                pool.tensor_tensor(e_rstd[n][:], e_mean_var[n][:, :, 1], e_ln_eps[:], ALU.add).then_inc(e_var_eps[n], 1)
                pool.wait_ge(e_var_eps[n], e.after(1, 1))
                pool.tensor_tensor(e_rstd[n][:], e_rstd[n][:], e_minus_half[:], ALU.pow).then_inc(e_rstd_done[n], 1)

            def add_b2(e):
                pool.wait_ge(x2_in, e.after(16, 16))
                pool.wait_ge(b2_in, e.after(16, 16))
                pool.wait_ge(xn_done, e.after(NM, NM))
                if e.n >= 1:
                    pool.wait_ge(e_res_done, e.after(NM, 0))
                else:
                    pool.wait_ge(u_done, NT * B)
                pool.tensor_tensor(x2b[:], x2[:], b2_all[:].broadcast_to([P, NM, D]), ALU.add).then_inc(x2b_half, 1)
                pool.wait_ge(x2b_half, e.after(1, 1))
                pool.tensor_tensor(x2b[:], x2b[:], x2[:], ALU.add).then_inc(x2b_done, 1)

            def first_w1_low():
                pool.wait_ge(w1_hi_done, 1)
                pool.tensor_tensor(w1_lo[0], w1_raw[0], w1_hi[0].bitcast(F32), ALU.subtract).then_inc(w1_lo_done, 1)

            def split_w2(e, s):
                e, s = slab(e, s)
                pool.wait_ge(w2_hi_done, e.after(SC, s + 1))
                pool.tensor_tensor(w2_lo[s % 2][:], w2_raw[s % 2][:], w2_hi[s % 2][:].bitcast(F32), ALU.subtract)\
                    .then_inc(w2_lo_done, 1)

            def expert(e, more):
                if e.n >= 1:
                    expert_scale(e - 1, 1)
                add_b2(e)
                for s in range(SC):
                    if more or s + 1 < SC:
                        split_w2(e, s + 1)
                    if s == 1 and more:
                        expert_scale(e + 1, 0)

            steps(pool, body)
            expert(Step(0), True)
            with pool.Fori(0, E - 2) as i:
                expert(Step(1, i), True)
            expert(Step(E - 1), False)
            last = Step(E - 1)
            for m in range(NM):
                pool.wait_ge(e_mean_done[1], last.after(NM, m + 1))
                scale = e_rstd[1][:, m:m + 1]
                pool.tensor_tensor(scale, e_mean_var[1][:, m, 1:2], e_ln_eps[:, m:m + 1], ALU.add).then_inc(e_var_eps[1], 1)
                pool.wait_ge(e_var_eps[1], last.after(1, m + 1))
                pool.tensor_tensor(scale, scale, e_minus_half[:, m:m + 1], ALU.pow).then_inc(e_rstd_done[1], 1)

        @block.vector
        def _(dve):
            dve.wait_ge(const_in, 16 * CONSTS)
            for k in range(KC):
                dve.wait_ge(w_hi, k + 1)
                dve.scalar_tensor_tensor(out=wg_lo[:, k, :], in0=wg_raw[:, k, :], scalar=normw[:, k:k + 1],
                                         in1=wg_hi[:, k, :].bitcast(F32), op0=ALU.mult, op1=ALU.subtract).then_inc(w_lo, 1)

            def weights_low(n, ks=range(KC)):
                for k in ks:
                    dve.wait_ge(w_hi, KC + (1, 2, 0, 3)[n] * KC + k + 1)
                    if n < 3:
                        cols = slice(n * D, (n + 1) * D)
                        dve.scalar_tensor_tensor(out=wqkv_lo[:, k, cols], in0=w_raw[n][:, k, :], scalar=normw[:, k:k + 1],
                                                 in1=wqkv_hi[:, k, cols].bitcast(F32), op0=ALU.mult,
                                                 op1=ALU.subtract).then_inc(w_lo, 1)
                    else:
                        dve.tensor_tensor(wout_lo[:, k, :], wout_raw[:, k, :], wout_hi[:, k, :].bitcast(F32),
                                          ALU.subtract).then_inc(w_lo, 1)

            def scale_h(b):
                dve.wait_ge(rms_done, b.after(1, 1))
                dve.wait_ge(x_in[b.odd], b.pair(16, 16))
                if b.n >= 1:
                    dve.wait_ge(h_turned, (b - 1).after(NT, NT))
                for j in range(NT):
                    dve.tensor_scalar(h[:, j, :], x_sb[b.odd][:, j, :], rms[:, j:j + 1], float(D) ** 0.5,
                                      ALU.mult, ALU.mult).then_inc(h_done, 1)

            def h_low(b):
                for j in range(NT):
                    dve.wait_ge(hT_hi_done, b.after(NT, j + 1))
                    cols = slice(j * P, (j + 1) * P)
                    dve.tensor_tensor(hT_lo[:, :, cols], turn[j][:].rearrange("p (k t) -> p k t", k=KC),
                                      hT_hi[:, :, cols].bitcast(F32), ALU.subtract).then_inc(hT_lo_done, 1)

            def sum_gates(b):
                dve.wait_ge(gates_low_out, b.after(1, 1))
                if b.n >= 1:
                    dve.wait_ge(gates_done, (b - 1).after(1, 1))
                dve.tensor_tensor(gates_sum[:], gate_ps[0:NG, 0:L], gates_low[:], ALU.add).then_inc(gates_summed, 1)

            def token_gates(b):
                dve.wait_ge(gates_turned, b.after(1, 1))
                if b.n >= 1:
                    dve.wait_ge(v_done, (b - 1).after(NT, NT))
                if b.n >= 2:
                    dve.wait_ge(qo_done, (b - 2).after(NT, NT))
                tok = gate_ps[:, L:L + NT * NG].rearrange("p (j g) -> p j g", g=NG)
                dve.tensor_scalar(g_tok[:], tok[:, :, NH:2 * NH], float(DH) ** -0.5, None, ALU.mult).then_inc(gates_tok, 1)
                dve.tensor_copy(o_tok[:, b.odd], tok[:, :, 2 * NH:NG]).then_inc(gates_tok, 1)

            def scan(b, n):
                dve.wait_ge(f_in, b.after(16, 16))
                if b.n == 0 and n == 0:
                    dve.wait_ge(ident_made, 3)
                if b.n >= 2 and n == 0:
                    dve.wait_ge(probs_done, (b - 2).after(NH, NH))
                dve.tensor_tensor_scan(decays[:, b.odd, n, P:DW], f_all[:, n, :], diag[:, P:DW], 0.0, ALU.mult, ALU.add)
                dve.tensor_tensor_scan(decays[:, b.odd, n, 0:P], f_all[:, n, P:L], diag[:, 0:P], 0.0, ALU.mult, ALU.add)\
                    .then_inc(decay_done, 1)

            def gate_v(b, j):
                dve.wait_ge(v_mm, b.after(NT, j + 1))
                dve.wait_ge(gates_tok, b.after(2, 2))
                if b.n >= 2 and j == 0:
                    dve.wait_ge(y_mm, (b - 2).after(KC, KC))
                dve.tensor_tensor(v_sb[b.odd][:, j, :].rearrange("p (h d) -> p h d", h=NH),
                                  v_ps[:].rearrange("p (h d) -> p h d", h=NH),
                                  g_tok[:, j, :].unsqueeze(2).broadcast_to([P, NH, DH]), ALU.mult).then_inc(v_done, 1)

            def rope_parts(b, j):
                dve.wait_ge(qk_mm, b.after(NT, j + 1))
                if b.n >= 1:
                    dve.wait_ge(qk_turned, (b - 1).after(2 * NT, 2 * NT))
                src = qk_ps[:].rearrange("p (h d) -> p h d", d=DH)
                a = rot_a[j].rearrange("p (h d) -> p h d", d=DH)
                s = rot_b[j].rearrange("p (h d) -> p h d", d=DH)

                def table(lo, hi):
                    return rope_sb[:, j:j + 1, lo:hi].broadcast_to([P, 2 * NH, hi - lo])

                dve.tensor_tensor(a, src, table(0, DH), ALU.mult)
                dve.tensor_tensor(s[:, :, 0:HALF], src[:, :, HALF:DH], table(DH, DH + HALF), ALU.mult)
                dve.tensor_tensor(s[:, :, HALF:DH], src[:, :, 0:HALF], table(DH + HALF, 2 * DH), ALU.mult).then_inc(rope_done, 1)

            def weigh(b, n):
                dve.wait_ge(s_mm, b.after(NH, n + 1))
                dve.wait_ge(decay_done, b.after(NH, n + 1))
                if n >= 4:
                    dve.wait_ge(y_mm, b.after(KC, (n - 4) // 2 + 1))
                elif b.n >= 1:
                    dve.wait_ge(y_mm, (b - 1).after(KC, (n + 4) // 2 + 1))
                dve.tensor_tensor(probs[:, n % 4, :], score_banks(b)[n % 2][:, 0:DW], decays[:, b.odd, n, :], ALU.mult).then_inc(probs_done, 1)

            def y_low(b, c):
                dve.wait_ge(y_hi_done, b.after(KC, c + 1))
                dve.tensor_tensor(yT_lo[:, c, :], y_ps[:, 0:L], yT_hi[:, c, :].bitcast(F32),
                                  ALU.subtract).then_inc(y_lo_done, 1)

            def add_residual(b):
                if b.n >= 1:
                    dve.wait_ge(x2_stored, (b - 1).after(16, 16))
                dve.wait_ge(xb_done, b.after(1, 1))
                for j in range(NT):
                    dve.wait_ge(out_mm, b.after(NT, j + 1))
                    dve.tensor_tensor(res[:, j, :], out_ps[j][:], xb[b.odd][:, j, :], ALU.add).then_inc(res_done, 1)

            def norm_stats(b, n):
                made, seen = ((res_done, stats_done), (u_done, stats2_done))[n]
                for j in range(NT):
                    dve.wait_ge(made, b.after(NT, j + 1))
                    dve.bn_stats(stats[:, j, :], res[:, j, :]).then_inc(seen, 1)
                dve.wait_ge(seen, b.after(NT, NT))
                dve.memset(moment[:], 0.0)
                for j in range(NT):
                    dve.bn_aggr(mean_var[n][:, j, :], stats[:, j, :]).then_inc(mean_done[n], 1)

            def normalize(b, n):
                dve.wait_ge(rstd_done[n], b.after(1, 1))
                for j in range(NT):
                    dve.tensor_scalar(res[:, j, :], res[:, j, :], mean_var[n][:, j, 0:1], rstd[n][:, j:j + 1],
                                      ALU.subtract, ALU.mult).then_inc((x1_done, x2_done)[n], 1)

            def add_memory(b):
                for j in range(NT):
                    dve.wait_ge(mem_grown, b.after(NT, j + 1))
                    dve.wait_ge(x1_done, b.after(NT, j + 1))
                    dve.tensor_tensor(res[:, j, :], c_sb[b.odd][:, j, :], res[:, j, :], ALU.mult).then_inc(u_done, 1)

            def body(b):
                if b.n == B:
                    expert_normalize(Step(0), 0)
                if b.n == B + 1:
                    add_memory(b - 2)
                    norm_stats(b - 2, 1)
                for n in range(NH):
                    if b.within(B) and n == 1:
                        token_gates(b)
                        gate_v(b, 0)
                    if b.within(B) and n == 5:
                        gate_v(b, 1)
                    if b.n == B and n in (2, 4, 6):
                        y_low(b - 1, n // 2 - 1)
                    if (b - 1).within(B) and n % 2 == 0:
                        weigh(b - 1, n)
                        weigh(b - 1, n + 1)
                    if (b - 1).within(B) and b.n != B and n in (3, 5, 7):
                        y_low(b - 1, (n - 3) // 2)
                    if b.n == B:
                        first_tokens(n)
                    if (b - 2).within(B) and b.n <= B:
                        if n == 1:
                            add_memory(b - 2)
                            norm_stats(b - 2, 1)
                        if n == 4:
                            normalize(b - 2, 1)
                    if b.n == 0 and n == 0:
                        weights_low(1)
                        dve.wait_ge(w_lo, W_OF[1])
                    if (b + 1).within(B) and n == 6:
                        scale_h(b + 1)
                    if b.within(B) and n == 3:
                        rope_parts(b, 0)
                    if b.within(B):
                        for m in SCANS.get(n, ()):
                            if b.n != 0 or m < 6:
                                scan(b, m)
                    if b.n == 0 and n >= NH - KC:
                        weights_low(3, [n - (NH - KC)])
                    if b.n == 0 and n == 7:
                        h_low(b + 1)
                    if b.within(B) and n == 7:
                        rope_parts(b, 1)
                        if b.n == 0:
                            scan(b, 6)
                            scan(b, 7)
                if b.n == B + 1:
                    normalize(b - 2, 1)
                if (b - 1).within(B):
                    y_low(b - 1, KC - 1)
                if (b + 1).within(B) and b.n != 0:
                    h_low(b + 1)
                if b.n == -1:
                    weights_low(2)
                if b.n == B - 1:
                    expert_stats(Step(0), 0)
                if b.n == -1:
                    sum_gates(b + 1)
                if (b - 1).within(B):
                    add_residual(b - 1)
                    if b.n == B:
                        split_hidden(Step(0), 0)
                    norm_stats(b - 1, 0)
                if (b + 1).within(B) and b.n >= 0:
                    sum_gates(b + 1)
                if b.n == B:
                    split_hidden(Step(0), 1)
                if (b - 1).within(B):
                    normalize(b - 1, 0)
                if b.n == -1:
                    weights_low(0)
                    dve.wait_ge(tables_in, 16 * 3)
                    dve.tensor_copy(sums[:].rearrange("p a t -> p (a t)"), memory_raw[:, 0:2 * P]).then_inc(sums_made, 1)

            def expert_stats(e, n):
                src = (x2, e_res)[n]
                if n == 0:
                    dve.wait_ge(x2_in, e.after(16, 16))
                for m in range(NM):
                    if n == 1:
                        dve.wait_ge(e_res_done, e.after(NM, m + 1))
                    dve.bn_stats(e_stats[n][:, m, :], src[:, m, :]).then_inc(e_stats_done[n], 1)
                dve.wait_ge(e_stats_done[n], e.after(NM, NM))
                dve.memset(moment[:], 0.0)
                for m in range(NM):
                    dve.bn_aggr(e_mean_var[n][:, m, :], e_stats[n][:, m, :]).then_inc(e_mean_done[n], 1)

            def expert_normalize(e, n):
                src, dst = ((x2, xn), (e_res, e_res))[n]
                dve.wait_ge(e_rstd_done[n], e.after(1, 1))
                if n == 0 and e.n >= 1:
                    dve.wait_ge(xn_turned, e.after(KC, 0))
                elif n == 0:
                    dve.wait_ge(qk_turned, 2 * NT * B)
                for m in range(NM):
                    dve.tensor_scalar(dst[:, m, :], src[:, m, :], e_mean_var[n][:, m, 0:1], e_rstd[n][:, m:m + 1],
                                      ALU.subtract, ALU.mult).then_inc((xn_done, out_done)[n], 1)

            def affine(e, k):
                dve.wait_ge(xn_turned, e.after(KC, k + 1))
                if e.n >= 1 and k == 0:
                    dve.wait_ge(xnT_hi_done, e.after(KC, 0))
                    dve.wait_ge(xnT_lo_done, e.after(KC, 0))
                dve.tensor_scalar(xnT[:, k, :], turn[k % 2][:], gamma_sb[:, k:k + 1], beta_sb[:, k:k + 1],
                                  ALU.mult, ALU.add).then_inc(xnT_done, 1)

            def token_low(e, k):
                dve.wait_ge(xnT_hi_done, e.after(KC, k + 1))
                dve.tensor_tensor(xnT_lo[:, k, :], xnT[:, k, :], xnT_hi[:, k, :].bitcast(F32), ALU.subtract)\
                    .then_inc(xnT_lo_done, 1)

            def split_w1(e, s):
                e, s = slab(e, s)
                dve.wait_ge(w1_hi_done, e.after(SC, s + 1))
                dve.tensor_tensor(w1_lo[s % 2][:], w1_raw[s % 2][:], w1_hi[s % 2][:].bitcast(F32), ALU.subtract)\
                    .then_inc(w1_lo_done, 1)

            def split_hidden(e, c):
                dve.wait_ge(gelu_done, e.after(FC, c + 1))
                if (c >= 2 or e.n >= 1) and not late(e, c):
                    dve.wait_ge(down_mm, e.after(FC, c - 1))
                high, low = hidden_parts(e, c)
                dve.tensor_copy(high, hid[c % 2][:]).then_inc(hid_hi_done, 1)
                dve.wait_ge(hid_hi_done, e.after(FC, c + 1))
                dve.tensor_tensor(low, hid[c % 2][:], high.bitcast(F32), ALU.subtract).then_inc(hid_lo_done, 1)

            def finish(e):
                dve.wait_ge(out_stored, e.after(16, 0))
                for m in range(NM):
                    dve.wait_ge(tile_mm, m + 1)
                    dve.tensor_tensor(e_res[:, m, :], acc[m][:], x2b[:, m, :], ALU.add).then_inc(e_res_done, 1)
                    dve.wait_ge(e_res_done, e.after(NM, m + 1))
                    dve.bn_stats(e_stats[1][:, m, :], e_res[:, m, :]).then_inc(e_stats_done[1], 1)
                    dve.wait_ge(e_stats_done[1], e.after(NM, m + 1))
                    dve.bn_aggr(e_mean_var[1][:, m, :], e_stats[1][:, m, :]).then_inc(e_mean_done[1], 1)
                    if m >= 1:
                        finish_norm(e, m - 1)
                finish_norm(e, NM - 1)

            def finish_norm(e, m):
                dve.wait_ge(e_rstd_done[1], e.after(1, m + 1))
                dve.tensor_scalar(e_res[:, m, :], e_res[:, m, :], e_mean_var[1][:, m, 0:1], e_rstd[1][:, m:m + 1],
                                  ALU.subtract, ALU.mult).then_inc(out_done, 1)

            def expert_residual(e):
                dve.wait_ge(down_mm, e.after(FC, FC))
                dve.wait_ge(x2b_done, e.after(1, 1))
                if e.n >= 1:
                    dve.wait_ge(out_stored, e.after(16, 0))
                for m in range(NM):
                    dve.tensor_tensor(e_res[:, m, :], acc[m][:], x2b[:, m, :], ALU.add).then_inc(e_res_done, 1)

            def first_tokens(n):
                if n == 0:
                    dve.wait_ge(e_const_in, 16 * 3)
                if n in (3, 5):
                    token_low(Step(0), n - 3)
                    token_low(Step(0), n - 2)

            def expert(e, more):
                for c in range(FC):
                    if c == FC - 1 and more:
                        for k in range(KC):
                            token_low(e + 1, k)
                    if c >= 2 or e.n >= 1:
                        split_hidden(e, c)
                    if e.n >= 1:
                        if c == 0:
                            expert_residual(e - 1)
                        if c == 1:
                            expert_stats(e - 1, 1)
                        if c == 3:
                            expert_normalize(e - 1, 1)
                    if c % CS == 2 and (more or c // CS + 1 < SC):
                        split_w1(e, c // CS + 1)
                    if more:
                        if c == 8:
                            expert_stats(e + 1, 0)
                        if c == 9:
                            expert_normalize(e + 1, 0)
                        if 11 <= c < 11 + KC:
                            affine(e + 1, c - 11)

            steps(dve, body)
            expert(Step(0), True)
            expert(Step(1), True)
            with dve.Fori(0, E - 3) as i:
                expert(Step(2, i), True)
            expert(Step(E - 1), False)
            finish(Step(E - 1))

        @block.tensor
        def _(pe):
            pe.wait_ge(ident_made, 1)
            for _ in range(WARM_UP):
                pe.matmul(gate_ps[:, 0:P], ident[:], ident[:], start=True, stop=True)

            def turn_h(b):
                if b.n >= 2:
                    pe.wait_ge(probs_done, (b - 2).after(NH, NH))
                else:
                    pe.wait_ge(ident_made, 3)
                for j in range(NT):
                    pe.wait_ge(h_done, b.after(NT, j + 1))
                    for k in range(KC):
                        mm = pe.transpose(turn[j][:, k * P:(k + 1) * P], h[:, j, k * P:(k + 1) * P], ident[:])
                    mm.then_inc(h_turned, 1)

            def gate_products(b):
                if b.n == 0:
                    pe.wait_ge(w_lo, W_GATES)
                    pe.wait_ge(wg_zero, 1)
                else:
                    pe.wait_ge(gates_tok, (b - 1).after(2, 2))
                pe.wait_ge(hT_lo_done, b.after(NT, NT))
                pe.matmul(gate_ps[0:LOW_ROW + NG, 0:L], wg_parts[:, 0, :], hT_hi[:, 0, :], start=True, stop=False)
                for k in range(KC):
                    pe.matmul(gate_ps[0:NG, 0:L], wg_hi[:, k, :], hT_lo[:, k, :], start=False, stop=False)
                for k in range(1, KC):
                    mm = pe.matmul(gate_ps[0:LOW_ROW + NG, 0:L], wg_parts[:, k, :], hT_hi[:, k, :],
                                   start=False, stop=k == KC - 1)
                mm.then_inc(gates_ps, 1)

            def turn_gates(b):
                pe.wait_ge(gates_done, b.after(1, 1))
                for j in range(NT):
                    mm = pe.matmul(gate_ps[:, L + j * NG:L + (j + 1) * NG], gates[:, j * P:(j + 1) * P],
                                   ident[0:NG, 0:NG], start=True, stop=True)
                mm.then_inc(gates_turned, 1)

            def project_share(b, g):
                j, n, k = g // (3 * KC), (2, 0, 1)[g // KC % 3], g % KC
                dst = v_ps[:] if n == 2 else qk_ps[:, n * D:(n + 1) * D]
                if k == 0 and n == 2 and j == 0:
                    if b.n >= 1:
                        pe.wait_ge(v_done, (b - 1).after(NT, NT))
                elif k == 0 and n == 2:
                    pe.wait_ge(v_done, b.after(NT, 1))
                elif k == 0 and n == 0 and j == 0 and b.n >= 2:
                    pe.wait_ge(mem_grown, (b - 2).after(NT, NT))
                elif k == 0 and n == 0 and j == 1:
                    pe.wait_ge(rope_done, b.after(NT, 1))
                if b.n == 0 and k == 0 and j == 0:
                    pe.wait_ge(w_lo, W_OF[n])
                tok = slice(j * P, (j + 1) * P)
                mm = exact_product(pe, dst, hT_hi[:, k, tok], hT_lo[:, k, tok],
                                   wqkv_hi[:, k, n * D:(n + 1) * D], wqkv_lo[:, k, n * D:(n + 1) * D],
                                   k == 0, k == KC - 1)
                if k == KC - 1 and n == 2:
                    mm.then_inc(v_mm, 1)
                if k == KC - 1 and n == 1:
                    mm.then_inc(qk_mm, 1)

            def turn_qk(b, j):
                pe.wait_ge(qo_done, b.after(NT, j + 1))
                for n in range(2):
                    if j == 1:
                        pe.wait_ge(qkT_done, b.after(2 * NT, n + 1))
                    elif (b + 1).within(B):
                        pe.wait_ge(hT_lo_done, (b + 1).after(NT, NT))
                    for k in range(KC):
                        mm = pe.transpose(turn[n][:, k * P:(k + 1) * P],
                                          rot_a[j][:, n * D + k * P:n * D + (k + 1) * P], ident[:])
                    mm.then_inc(qk_turned, 1)

            def scores(b, c):
                if c == 0:
                    pe.wait_ge(qkT_done, b.after(2 * NT, 2 * NT))
                if c >= 1:
                    pe.wait_ge(probs_done, b.after(NH, 2 * c))
                elif b.n == B - 1 and b.i is None:
                    pe.wait_ge(res_done, (b - 1).after(NT, 1))
                    pe.wait_ge(gates_tok, b.after(2, 2))
                halves = (slice(0, DH), slice(DH, 2 * DH))
                for rows, bank in zip(halves, score_banks(b)):
                    pe.matmul(bank[:, 0:P], kT[rows, c, P:L], qT[rows, c, P:L], start=True, stop=True)
                for rows, bank in zip(halves, score_banks(b)):
                    pe.matmul(bank[:, P:DW], kT[rows, c, 0:P], qT[rows, c, 0:L], start=True, stop=True).then_inc(s_mm, 1)

            def weighted_values(b, c):
                if c >= 1:
                    pe.wait_ge(y_lo_done, b.after(KC, c))
                elif b.n >= 1:
                    pe.wait_ge(res_done, (b - 1).after(NT, NT))
                v = v_sb[b.odd]
                pe.wait_ge(probs_done, b.after(NH, 2 * c + 2))
                for n in (2 * c, 2 * c + 1):
                    rows = slice(n % 2 * DH, (n % 2 + 1) * DH)
                    pe.matmul(y_ps[rows, 0:L], v[:, 0, n * DH:(n + 1) * DH], probs[:, n % 4, P:DW],
                              start=True, stop=False)
                for n in (2 * c, 2 * c + 1):
                    rows = slice(n % 2 * DH, (n % 2 + 1) * DH)
                    mm = pe.matmul(y_ps[rows, P:L], v[:, 1, n * DH:(n + 1) * DH], probs[:, n % 4, 0:P],
                                   start=False, stop=True)
                mm.then_inc(y_mm, 1)

            def slot(b, n):
                if b.within(B):
                    project_share(b, 3 * n)
                    project_share(b, 3 * n + 1)
                if (b - 1).within(B) and (n % 2 == 0 and (b.n, n) != (1, 0) or (b.n, n) == (1, 1)):
                    scores(b - 1, n // 2)
                if b.n == B and n < KC:
                    turn_tokens(Step(0), n)
                elif b.n == B:
                    up(Step(0), 0, n - KC)
                if (b - 1).within(B) and b.n != B and n in (2, 4, 6):
                    weighted_values(b - 1, n // 2 - 1)
                if b.within(B):
                    project_share(b, 3 * n + 2)
                    if n == 0:
                        turn_gates(b)
                if (b.n, n) == (1, 0):
                    turn_qk(b - 1, 1)
                if (b - 1).within(B) and (n == NH - 1 or b.n == B and n % 2 == 1):
                    weighted_values(b - 1, n // 2)

            def project_out(b):
                if b.n == 0:
                    pe.wait_ge(w_lo, W_OUT)
                for j in range(NT):
                    if j == 0 and b.n == B - 1 and b.i is None:
                        pe.wait_ge(probs_done, b.after(NH, NH))
                    elif j == 0 and b.n >= 1:
                        pe.wait_ge(res_done, (b - 1).after(NT, 1))
                    for k in range(KC):
                        if j == 0:
                            pe.wait_ge(y_lo_done, b.after(KC, k + 1))
                        tok = slice(j * P, (j + 1) * P)
                        mm = exact_product(pe, out_ps[j][:], yT_hi[:, k, tok], yT_lo[:, k, tok],
                                           wout_hi[:, k, :], wout_lo[:, k, :], k == 0, k == KC - 1)
                    mm.then_inc(out_mm, 1)

            def cross_memory(b):
                if b.n == 0:
                    pe.wait_ge(sums_made, 1)
                pe.wait_ge(ctx_lo_done, b.after(1, 1))
                if (b + 1).within(B):
                    pe.wait_ge(rope_done, (b + 1).after(NT, NT))
                now, later = memory(b)
                pe.matmul(now, sums[:, 0, :], ctx_hi[:, 0, :], start=True, stop=False)
                pe.matmul(now, sums[:, 0, :], ctx_lo[:, 0, :], start=False, stop=True).then_inc(mem_mm, 1)
                pe.matmul(later, sums[:, 0, :], ctx_hi[:, 1, :], start=True, stop=False)
                pe.matmul(later, sums[:, 0, :], ctx_lo[:, 1, :], start=False, stop=False)
                pe.matmul(later, sums[:, 1, :], ctx_hi[:, 0, :], start=False, stop=False)
                pe.matmul(later, sums[:, 1, :], ctx_lo[:, 0, :], start=False, stop=True).then_inc(mem_mm, 1)

            def body(b):
                for n in range(NH):
                    slot(b, n)
                if (b + 1).within(B):
                    turn_h(b + 1)
                if b.n == B:
                    cross_memory(b - 1)
                if (b - 1).within(B):
                    project_out(b - 1)
                if (b + 1).within(B):
                    gate_products(b + 1)
                if b.within(B):
                    turn_qk(b, 0)
                if (b - 1).within(B) and b.n != B:
                    cross_memory(b - 1)
                if b.within(B) and b.n != 0:
                    turn_qk(b, 1)

            def turn_tokens(e, k):
                if k == 0:
                    pe.wait_ge(xn_done, e.after(NM, NM))
                if k >= 2 or e.n >= 1:
                    pe.wait_ge(xnT_done, e.after(KC, k - 1))
                for m in range(NM):
                    mm = pe.transpose(turn[k % 2][:, m * P:(m + 1) * P], xn[:, m, k * P:(k + 1) * P], ident[:])
                mm.then_inc(xn_turned, 1)

            def up(e, c, k):
                s = c // CS
                if k == 0:
                    if c % CS == 0:
                        pe.wait_ge(w1_lo_done, e.after(SC, s + 1))
                    if c >= 2 or e.n >= 1:
                        pe.wait_ge(gelu_done, e.after(FC, c - 1))
                    elif c == 0:
                        pe.wait_ge(v_done, NT * B)
                    else:
                        pe.wait_ge(probs_done, NH * B)
                if c == 0:
                    pe.wait_ge(xnT_lo_done, e.after(KC, k + 1))
                cols = slice(c % CS * P, (c % CS + 1) * P)
                mm = exact_product(pe, up_ps[c % 2][:], w1_hi[s % 2][:, k, cols], w1_lo[s % 2][:, k, cols],
                                   xnT_hi[:, k, :], xnT_lo[:, k, :], k == 0, k == KC - 1)
                if k == KC - 1:
                    mm.then_inc(up_mm, 1)

            def down_share(e, c, m):
                s, tok = c // CS, slice(m * P, (m + 1) * P)
                high, low = hidden_parts(e, c)
                return exact_product(pe, acc[m][:], high[:, tok], low[:, tok],
                                     w2_hi[s % 2][:, c % CS, :], w2_lo[s % 2][:, c % CS, :], c == 0, c == FC - 1)

            def down(e, c):
                if c % CS == 0:
                    pe.wait_ge(w2_lo_done, e.after(SC, c // CS + 1))
                pe.wait_ge(hid_lo_done, e.after(FC, c + 1))
                for m in range(NM):
                    if c == 0 and e.n >= 1:
                        pe.wait_ge(e_res_done, e.after(NM, m + 1 - NM))
                    elif c == 0 and m < NT:
                        pe.wait_ge(res_done, NT * (B - 1) + m + 1)
                    elif c == 0:
                        pe.wait_ge(mem_grown, NT * (B - 1))
                    mm = down_share(e, c, m)
                mm.then_inc(down_mm, 1)

            def down_tiles(e):
                pe.wait_ge(w2_lo_done, e.after(SC, SC))
                for m in range(NM):
                    for c in range(FC - CS, FC):
                        if m == 0:
                            pe.wait_ge(hid_lo_done, e.after(FC, c + 1))
                        mm = down_share(e, c, m)
                    mm.then_inc(tile_mm, 1)

            def expert(e, more):
                for c in range(1, FC):
                    for k in range(KC):
                        up(e, c, k)
                    if not late(e, c - 1):
                        down(e, c - 1)
                    if more and 11 <= c < 11 + KC:
                        turn_tokens(e + 1, c - 11)
                if more:
                    for k in range(KC):
                        up(e + 1, 0, k)
                    down(e, FC - 1)
                else:
                    down_tiles(e)

            steps(pe, body)
            expert(Step(0), True)
            with pe.Fori(0, E - 2) as i:
                expert(Step(1, i), True)
            expert(Step(E - 1), False)


def rope_tables():
    half = np.arange(HALF, dtype=np.float32) / np.float32(HALF)
    inv_freq = np.float32(1.0) / np.float32(THETA) ** half
    angles = np.arange(L, dtype=np.float32)[:, None] * inv_freq[None, :]
    cos, sin = np.cos(angles), np.sin(angles)
    return np.ascontiguousarray(np.concatenate([cos, cos, -sin, sin], axis=1), np.float32)


def decay_tables():
    upper = np.triu(np.ones((P, P)))
    t = np.arange(P)[:, None] + P * np.arange(NT)[None, :]
    t = t - P
    base = float(np.float32(DECAY))
    return np.ascontiguousarray(np.concatenate([upper, np.ones((P, P)), base ** (-t / 2), base ** t], axis=1), np.float32)


def kernel(**inputs):
    import concourse.bacc as _bacc
    from concourse.bass_utils import run_bass_kernel_spmd as _run

    def arr(name):
        return np.ascontiguousarray(inputs[name])

    def turned(name):
        return np.ascontiguousarray(np.asarray(inputs[name]).T)

    def columns(name):
        return np.ascontiguousarray(np.asarray(inputs[name]).reshape(-1, P).T)

    a = "L0_attn_"
    f = "L0_ffn_"
    arrays = {
        "x": arr("x"), "ctx_in": arr("ctx_1024"), "norm_w": columns(a + "norm_w"),
        "wqT": turned(a + "Wq"), "wkT": turned(a + "Wk"), "wvT": turned(a + "Wv"),
        "wbetaT": turned(a + "Wbeta"), "bbeta": arr(a + "bbeta"), "wigT": turned(a + "Wig"), "big": arr(a + "big"),
        "wogT": turned(a + "Wog"), "bog": arr(a + "bog"), "woutT": turned(a + "Wout"), "bout": arr(a + "bout"),
        "gamma": columns(f + "gamma"), "beta": columns(f + "beta"), "w1": arr(f + "w1"), "b1": columns(f + "b1"),
        "w2": arr(f + "w2"), "b2": arr(f + "b2"), "rope": rope_tables(), "decay": decay_tables(),
    }
    nc = _bacc.Bacc("TRN2", target_bir_lowering=False, num_devices=1)
    aps = {k: nc.dram_tensor(f"in_{k}", v.shape, mybir.dt.from_np(v.dtype), kind="ExternalInput").ap()
           for k, v in arrays.items()}
    out = nc.dram_tensor("out_0", (B, L, D), F32, kind="ExternalOutput").ap()
    decoder_layer(nc, out=out, **aps)
    r = _run(nc, [{f"in_{k}": v for k, v in arrays.items()}], core_ids=[0])
    return r.results[0]["out_0"]
```
